# Optimizing a Trainium2 kernel written in Bass

```python
import numpy as np
import jax
import jax.numpy as jnp

def _softmax(x, axis=-1):
    return jax.nn.softmax(x, axis=axis)

def _gelu(x):
    return jax.nn.gelu(x, approximate=True)

def _silu(x):
    return jax.nn.silu(x)

def _sigmoid(x):
    return jax.nn.sigmoid(x)

def _layernorm(x, axis=-1, eps=1e-05):
    m = jnp.mean(x, axis=axis, keepdims=True)
    v = jnp.var(x, axis=axis, keepdims=True)
    return (x - m) / jnp.sqrt(v + eps)

def _scatter_add(tgt, idx, src, axis=0):
    return tgt.at[idx].add(src)

def _segment_sum(src, seg, n):
    return jax.ops.segment_sum(src, seg, n)
kernel_name = 'mk_sandwich_d1_jaxref_r4_e9ebc0'

def setup_inputs(seed: int=0):
    np.random.seed(seed)
    _w = jnp.asarray

    def _L0_attn_setup():
        import jax, jax.numpy as jnp
        import numpy as np
        B, S, HIDDEN = (2, 512, 1024)
        TP = 2
        PART = HIDDEN // TP
        NUM_HEADS = 16 // TP
        HEAD_DIM = PART // NUM_HEADS
        MASKED_BIAS = -10000.0
        key = jax.random.key(seed)
        k_x, k_wq, k_bq, k_wo, k_bo = jax.random.split(key, 5)
        x = jax.random.normal(k_x, (B, S, HIDDEN), dtype=jnp.float32)
        w_qkv = jax.random.normal(k_wq, (3 * PART, HIDDEN), dtype=jnp.float32) * 0.02
        b_qkv = jax.random.normal(k_bq, (3 * PART,), dtype=jnp.float32) * 0.02
        w_o = jax.random.normal(k_wo, (HIDDEN, PART), dtype=jnp.float32) * 0.02
        b_o = jax.random.normal(k_bo, (HIDDEN,), dtype=jnp.float32) * 0.02
        return {'x': x, 'w_qkv': w_qkv, 'b_qkv': b_qkv, 'w_o': w_o, 'b_o': b_o}
    _L0_attn_in = _L0_attn_setup()

    def _L0_ffn_setup():
        import jax, jax.numpy as jnp
        import numpy as np
        RANKS = (8, 16, 32, 64)
        TOPK = 1
        SCALING = 1.0 / 4
        key = jax.random.key(seed)
        ks = jax.random.split(key, 7)
        D_IN, D_OUT, MAX_R, N_RANKS = (1024, 1024, 64, len(RANKS))
        B_, S_ = (4, 512)
        return {'hidden_states': jax.random.normal(ks[0], (B_, S_, D_IN), jnp.float32), 'W': jax.random.normal(ks[1], (D_OUT, D_IN), jnp.float32) * 0.02, 'b': jax.random.normal(ks[2], (D_OUT,), jnp.float32) * 0.02, 'A': jax.random.normal(ks[3], (MAX_R, D_IN), jnp.float32) * 0.02, 'B': jnp.zeros((D_OUT, MAX_R), jnp.float32) + jax.random.normal(ks[4], (D_OUT, MAX_R), jnp.float32) * 0.02, 'gate_w': jax.random.normal(ks[5], (N_RANKS, D_IN), jnp.float32) * 0.02, 'gate_b': jax.random.normal(ks[6], (N_RANKS,), jnp.float32) * 0.02}
    _L0_ffn_in = _L0_ffn_setup()
    _d = {'L0_attn_x': _L0_attn_in['x'], 'L0_attn_w_qkv': _L0_attn_in['w_qkv'], 'L0_attn_b_qkv': _L0_attn_in['b_qkv'], 'L0_attn_w_o': _L0_attn_in['w_o'], 'L0_attn_b_o': _L0_attn_in['b_o'], 'L0_ffn_W': _L0_ffn_in['W'], 'L0_ffn_b': _L0_ffn_in['b'], 'L0_ffn_A': _L0_ffn_in['A'], 'L0_ffn_B': _L0_ffn_in['B'], 'L0_ffn_gate_w': _L0_ffn_in['gate_w'], 'L0_ffn_gate_b': _L0_ffn_in['gate_b']}
    _x0 = _d['L0_attn_x']
    _d['L0_attn_x'] = jax.random.normal(jax.random.fold_in(jax.random.key(seed), 1), (8, 512, 1024), dtype=_x0.dtype)
    del _x0
    return _d

def reference(L0_attn_x, L0_attn_w_qkv, L0_attn_b_qkv, L0_attn_w_o, L0_attn_b_o, L0_ffn_W, L0_ffn_b, L0_ffn_A, L0_ffn_B, L0_ffn_gate_w, L0_ffn_gate_b):

    def _L0_attn_ref(x, w_qkv, b_qkv, w_o, b_o):
        import jax, jax.numpy as jnp
        import numpy as np
        B, S, HIDDEN = (2, 512, 1024)
        TP = 2
        PART = HIDDEN // TP
        NUM_HEADS = 16 // TP
        HEAD_DIM = PART // NUM_HEADS
        MASKED_BIAS = -10000.0
        b, s, _ = x.shape
        qkv = x @ w_qkv.T + b_qkv
        q, k, v = jnp.split(qkv, 3, axis=-1)

        def to_heads(a):
            return a.reshape(b, s, NUM_HEADS, HEAD_DIM).transpose(0, 2, 1, 3)
        q, k, v = (to_heads(q), to_heads(k), to_heads(v))
        scores = jnp.einsum('bhfc,bhtc->bhft', k, q)
        causal = jnp.triu(jnp.ones((s, s), dtype=bool))
        scores = jnp.where(causal[None, None], scores, MASKED_BIAS)
        attn = jax.nn.softmax(scores, axis=-2)
        vals = jnp.einsum('bhft,bhfc->bhtc', attn, v)
        vals = vals.transpose(0, 2, 1, 3).reshape(b, s, PART)
        out = vals @ w_o.T + b_o
        return out

    def _L0_ffn_ref(hidden_states, W, b, A, B, gate_w, gate_b):
        import jax, jax.numpy as jnp
        import numpy as np
        RANKS = (8, 16, 32, 64)
        TOPK = 1
        SCALING = 1.0 / 4
        bsz, seq, d_in = hidden_states.shape
        out = jnp.einsum('bsd,od->bso', hidden_states, W) + b
        x = hidden_states.reshape(-1, d_in)
        scores = x @ gate_w.T + gate_b
        probs = jax.nn.softmax(scores, axis=-1)
        routing_weights, selected = jax.lax.top_k(probs, TOPK)
        routing_weights = routing_weights / jnp.sum(routing_weights, axis=-1, keepdims=True)
        lora_outputs = jnp.stack([x @ A[:r, :].T @ B[:, :r].T for r in RANKS], axis=1)
        sel = jnp.take_along_axis(lora_outputs, selected[:, :, None], axis=1)
        final = jnp.sum(sel * routing_weights[:, :, None], axis=1)
        return out + final.reshape(bsz, seq, -1)
    x = L0_attn_x
    x = x + _layernorm(_L0_attn_ref(_layernorm(x, axis=-1), L0_attn_w_qkv, L0_attn_b_qkv, L0_attn_w_o, L0_attn_b_o), axis=-1)
    x = x + _layernorm(_L0_ffn_ref(_layernorm(x, axis=-1), L0_ffn_W, L0_ffn_b, L0_ffn_A, L0_ffn_B, L0_ffn_gate_w, L0_ffn_gate_b), axis=-1)
    return x

_drawn_inputs = setup_inputs


def setup_inputs(seed=0):
    import zlib

    import numpy as np

    out = dict(_drawn_inputs(seed))
    spreads = {}
    factors = {'L0_ffn_b': 3.238, 'L0_ffn_gate_b': 22.242}
    for name, (base, spread) in spreads.items():
        noise = np.random.default_rng([zlib.crc32(name.encode()), seed]).standard_normal(out[name].shape)
        drawn = base * np.exp(spread * noise) if base else spread * noise
        out[name] = jnp.asarray(drawn.astype(out[name].dtype))
    for name, factor in factors.items():
        out[name] = (out[name] * factor).astype(out[name].dtype)
    return out
```

```python
from contextlib import ExitStack

import concourse.bass as bass
from concourse import mybir

ALU = mybir.AluOpType
ACT = mybir.ActivationFunctionType
AX = mybir.AxisListType
F32 = mybir.dt.float32
F32R = mybir.dt.float32r
U32 = mybir.dt.uint32

P = 128
EPS = 1e-5
MASKED = -10000.0


def attention_phase(nc, x, wqkvT, bqk, bv, valsT):
    NB, S, D = x.shape
    E = wqkvT.shape[1]
    PART = E // 3
    HD = 64
    NH = PART // HD
    NPAIR = NH // 2
    KD = D // P
    NT = S // P
    assert NT == 4 and NH == 8 and S == 512

    PT_OFF = [0, 512, 896, 1152]
    PT_N = 1280
    PT_GROUP = [(0, 512), (512, 512), (1024, 256)]
    PT_BLOCKS = [(i, j, PT_OFF[j] + (i - j) * P) for j in range(NT) for i in range(j, NT)]
    S_OFF = {3: 0, 2: 512, 0: 896, 1: 1024}

    WHOLE, FIRST, SECOND = range(KD), range(KD // 2), range(KD // 2, KD)
    BETWEEN = [
        ([("v", 0, 0, WHOLE), ("v", 1, 0, WHOLE)], []),
        ([("v", 2, 0, WHOLE)], [("v", 3, 0, WHOLE)]),
        ([("k", 2, 0, WHOLE)], [("q", 2, 0, FIRST)]),
        ([("q", 2, 0, SECOND)], [("k", 3, 0, WHOLE)]),
        ([("q", 3, 0, WHOLE)], [("x", 0, 1, WHOLE)]),
        ([("x", 1, 1, WHOLE)], [("x", 2, 1, WHOLE)]),
        ([("x", 3, 1, WHOLE)], [("k", 0, 1, WHOLE)]),
        ([("q", 0, 1, FIRST)], [("q", 0, 1, SECOND)]),
        ([("k", 1, 1, WHOLE)], [("q", 1, 1, FIRST)]),
        ([("q", 1, 1, SECOND)], []),
    ]
    SLOTS = len(BETWEEN)
    EARLY = [("x", t, g) for t in range(NT) for g in range(2)] + [("k", 0), ("q", 0), ("k", 1), ("q", 1)]
    NOW = [("v", 0), ("v", 1), ("v", 2), ("v", 3), ("k", 2), ("q", 2), ("k", 3), ("q", 3)]

    with ExitStack() as ctx:
        def sb(name, shape, dt, c=ctx):
            return c.enter_context(nc.sbuf_tensor(name, shape, dt))

        def sem(name):
            return ctx.enter_context(nc.semaphore(name))

        with ExitStack() as early:
            raw = sb("raw", [P, 4, E], F32, early)
        qst = sb("qst", [P, 2, 2, S], F32R)
        kst = sb("kst", [P, 2, 2, 2, S], F32R)
        wh = sb("wh", [P, KD, E], F32R)
        wl = sb("wl", [P, KD, E], F32R)
        xTh = sb("xTh", [P, KD, S], F32R)
        xTl = sb("xTl", [P, KD, S], F32R)
        v = sb("v", [P, NT, NH, 2 * HD], F32R)
        PTh = sb("PTh", [P, PT_N], F32R)
        PTl = sb("PTl", [P, PT_N], F32R)
        WT = sb("WT", [P, 3 * P], F32R)
        Dw = sb("Dw", [P, 3 * P], F32R)
        ones = sb("ones", [P, P], F32R)
        xs = sb("xs", [P, 3, D], F32)
        pr = sb("pr", [P, 2, PT_N], F32)
        vt = sb("vt", [P, S], F32)
        ident = sb("ident", [P, P], F32)
        maskf = sb("maskf", [P, P], F32)
        masked = sb("masked", [P, 1], F32)
        cnt = sb("cnt", [P, 4], F32)
        bqk_s = sb("bqk_s", [P, 2 * NPAIR], F32)
        bv_s = sb("bv_s", [HD, NH], F32)
        stats = sb("stats", [P, 2, 12], F32)
        mv = sb("mv", [P, 2, 2], F32)
        var_eps = sb("var_eps", [P, 2], F32)
        rstd = sb("rstd", [P, 2], F32)
        nmean = sb("nmean", [P, 2], F32)
        mhalf = sb("mhalf", [P, 1], F32)
        mone = sb("mone", [P, 1], F32)
        eps = sb("eps", [P, 1], F32)
        hold = sb("hold", [1, 3], F32)
        nm = sb("nm", [P, 2, 4], F32)
        acc = sb("acc", [P, 2, 4], F32)
        wm = sb("wm", [P, 2, 4], F32)
        cw = sb("cw", [P, 2, 4], F32)
        den = sb("den", [P, 2, 4], F32)
        rden = sb("rden", [P, 2, 4], F32)
        wn = sb("wn", [P, 2, 4], F32)

        ps_s = ctx.enter_context(nc.psum_tensor("ps_s", [P, 3 * 512], F32))
        ps_t = [ctx.enter_context(nc.psum_tensor(f"ps_t{i}", [P, 512], F32)) for i in range(2)]
        ps_j = [ctx.enter_context(nc.psum_tensor(f"ps_j{i}", [P, 512], F32)) for i in range(2)]
        ps_v = ctx.enter_context(nc.psum_tensor("ps_v", [P, 512], F32))

        x_landed = [sem(f"x_landed{i}") for i in range(NT)]
        w_landed = [sem(f"w_landed{i}") for i in range(4)]
        bias_landed = sem("bias_landed")
        consts = sem("consts")
        w_hi = sem("w_hi")
        w_ready = sem("w_ready")
        mv_ready = sem("mv_ready")
        ve_done = sem("ve_done")
        xn_ready = sem("xn_ready")
        t_full = [sem(f"t_full{i}") for i in range(2)]
        t_hi = sem("t_hi")
        t_lo = sem("t_lo")
        wt_ready = sem("wt_ready")
        j_full = [sem(f"j_full{i}") for i in range(2)]
        j_hi = sem("j_hi")
        j_lo = sem("j_lo")
        k_dup = [sem(f"k_dup{i}") for i in range(2)]
        s_done = sem("s_done")
        held = sem("held")
        mask_done = sem("mask_done")
        max_done = sem("max_done")
        nm_ready = sem("nm_ready")
        exp_done = sem("exp_done")
        cw_done = sem("cw_done")
        den_ready = sem("den_ready")
        rden_ready = sem("rden_ready")
        wn_done = sem("wn_done")
        p_ready = sem("p_ready")
        d_ready = sem("d_ready")
        pv_done = sem("pv_done")
        vlo_done = sem("vlo_done")
        vals_ready = sem("vals_ready")
        vals_stored = sem("vals_stored")

        xf = x.rearrange("b s d -> (b s) d")
        vf = valsT.rearrange("b c t -> (b c) t")

        def x_slot(t):
            return t % 3

        def j_index(entry, b):
            if entry in EARLY:
                return 20 * b + EARLY.index(entry)
            return 20 * b + len(EARLY) + NOW.index(entry)

        def j_bank(entry):
            return j_index(entry, 0) % 2

        def j_uses(entry, b):
            return 10 * b + j_index(entry, 0) // 2 + 1

        def between(h, part, b, last):
            return [(kind, p, b + ahead, ks) for kind, p, ahead, ks in BETWEEN[h][part] if not (last and ahead)]

        block = ctx.enter_context(nc.Block())

        @block.sync
        def _(sp):
            def load_x(t, b):
                sp.dma_start(xs[:, x_slot(t), :], xf[bass.ds(b * S + t * P, P), :]).then_inc(x_landed[t], 16)

            def dup_k(p, b):
                sp.wait_ge(j_lo, j_index(("k", p), b) + 1)
                sp.dma_start(kst[HD:P, p % 2, 0, :, :].bitcast(F32), kst[0:HD, p % 2, 0, :, :].bitcast(F32)).then_inc(k_dup[p % 2], 16)
                sp.dma_start(kst[0:HD, p % 2, 1, :, :].bitcast(F32), kst[HD:P, p % 2, 1, :, :].bitcast(F32)).then_inc(k_dup[p % 2], 16)

            def store_vals(h, b):
                sp.wait_ge(vals_ready, 1 + 8 * b + h + 1)
                sp.dma_start(vf[bass.ds(b * PART + h * HD, HD), :], vt[0:HD, :]).then_inc(vals_stored, 16)

            def body(b, last):
                if not last:
                    sp.wait_ge(j_lo, j_index(("x", 3, 1), b) + 1)
                    for t in range(3):
                        load_x(t, b + 1)
                for h in range(SLOTS):
                    if h >= 2:
                        store_vals(h - 2, b)
                    if h in (2, 4):
                        dup_k(h // 2 + 1, b)
                    if h == 4 and not last:
                        sp.wait_ge(j_full[1], j_uses(("x", 0, 1), b + 1))
                        load_x(3, b + 1)
                    if h in (7, 8) and not last:
                        dup_k(h - 7, b + 1)

            for t in range(3):
                load_x(t, 0)
            sp.dma_start(bqk_s[:, :], bqk).then_inc(bias_landed, 16)
            sp.dma_start(bv_s[:, :], bv).then_inc(bias_landed, 16)
            for k in range(KD):
                if k >= 4:
                    sp.wait_ge(w_ready, k - 3)
                if k == 4:
                    sp.wait_ge(j_full[1], 1)
                    load_x(3, 0)
                sp.dma_start(raw[:, k % 4, :], wqkvT[k * P:(k + 1) * P, :]).then_inc(w_landed[k % 4], 16)
            dup_k(0, 0)
            dup_k(1, 0)
            with sp.Fori(0, NB - 1) as b:
                body(b, False)
            body(NB - 1, True)
            sp.wait_ge(vals_stored, 16 + 16 * NB * NH)

        @block.gpsimd
        def _(pool):
            def layernorm(t, b):
                n, q = 4 * b + t, t % 2
                pool.wait_ge(mv_ready, n + 1)
                pool.tensor_tensor(var_eps[:, q:q + 1], mv[:, q, 1:2], eps[:, :], ALU.add).then_inc(ve_done, 1)
                pool.tensor_tensor(nmean[:, q:q + 1], mv[:, q, 0:1], mone[:, :], ALU.mult)
                pool.wait_ge(ve_done, n + 1)
                pool.tensor_tensor(rstd[:, q:q + 1], var_eps[:, q:q + 1], mhalf[:, :], ALU.pow)
                pool.drain()
                at = xs[:, x_slot(t), :]
                pool.tensor_scalar(at, at, nmean[:, q:q + 1], rstd[:, q:q + 1], ALU.add, ALU.mult)\
                    .then_inc(xn_ready, 1)

            def normalise(h, b):
                H, q = 8 * b + h, h % 2
                pool.wait_ge(exp_done, H + 1)
                pool.tensor_tensor(cw[:, q, :], wm[:, q, :], cnt[:, :], ALU.mult).then_inc(cw_done, 1)
                pool.wait_ge(cw_done, H + 1)
                pool.tensor_tensor(den[:, q, :], cw[:, q, :], acc[:, q, :], ALU.add).then_inc(den_ready, 1)
                pool.wait_ge(rden_ready, H + 1)
                pool.tensor_tensor(wn[:, q, :], wm[:, q, :], rden[:, q, :], ALU.mult).then_inc(wn_done, 1)
                for i in range(NT):
                    at = pr[:, q, S_OFF[i]:S_OFF[i] + (i + 1) * P]
                    last = pool.tensor_scalar(at, at, rden[:, q, i:i + 1], 1.0, ALU.mult, ALU.mult)
                last.then_inc(p_ready, 1)
                pool.wait_ge(wn_done, H + 1)
                if h > 0:
                    pool.wait_ge(wt_ready, H)
                pool.tensor_tensor(Dw[:, :].rearrange("p (i t) -> p i t", i=3),
                                   ident[:, :].unsqueeze(1).to_broadcast([P, 3, P]),
                                   wn[:, q, 0:3].unsqueeze(2).to_broadcast([P, 3, P]), ALU.mult).then_inc(d_ready, 1)

            def body(b, last):
                for h in range(NH):
                    if h == 5 and not last:
                        layernorm(3, b + 1)
                    normalise(h, b)
                    if h < 3 and not last:
                        layernorm(h, b + 1)

            pool.memset(ident[:, :], 0.0).then_inc(consts, 1)
            pool.memset(maskf[:, :], 0.0).then_inc(consts, 1)
            pool.memset(mhalf[:, :], -0.5).then_inc(consts, 1)
            pool.memset(mone[:, :], -1.0).then_inc(consts, 1)
            pool.memset(eps[:, :], EPS).then_inc(consts, 1)
            pool.memset(masked[:, :], MASKED).then_inc(consts, 1)
            for i in range(NT):
                pool.memset(cnt[:, i:i + 1], float(S - (i + 1) * P)).then_inc(consts, 1)
            pool.memset(wm[:, :, :], 0.0).then_inc(consts, 1)
            pool.memset(ones[:, :].bitcast(F32), 1.0).then_inc(consts, 1)
            pool.memset(hold[:, 1:2], 0.0).then_inc(vals_ready, 1)
            pool.memset(hold[:, 2:3], 0.0).then_inc(vals_stored, 16)
            pool.memset(hold[:, 0:1], 0.0).then_inc(held, 1)
            pool.wait_ge(consts, 12)
            pool.affine_select(out=ident[:, :], in_=ident[:, :], compare_op=ALU.not_equal, fill=1.0, base=0,
                               pattern=[[-1, P]], channel_multiplier=1).then_inc(consts, 1)
            pool.affine_select(out=maskf[:, :], in_=maskf[:, :], compare_op=ALU.is_ge, fill=1.0, base=0,
                               pattern=[[-1, P]], channel_multiplier=1).then_inc(consts, 1)
            for t in range(NT):
                layernorm(t, 0)
            with pool.Fori(0, NB - 1) as b:
                body(b, False)
            body(NB - 1, True)

        @block.vector
        def _(dve):
            def layernorm_stats(t, b):
                q, s = t % 2, x_slot(t)
                dve.wait_ge(x_landed[t], 16 * (b + 1))
                if not (isinstance(b, int) and 4 * b + t < 2):
                    dve.wait_ge(xn_ready, 4 * b + t - 1)
                for i in range(2):
                    dve.bn_stats(stats[:, q, 6 * i:6 * i + 6], xs[:, s, 512 * i:512 * i + 512])
                dve.drain()
                dve.bn_aggr(mv[:, q, :], stats[:, q, :]).then_inc(mv_ready, 1)

            def x_lo(t, b):
                for g in range(2):
                    dve.wait_ge(j_hi, j_index(("x", t, g), b) + 1)
                    at = (slice(None), slice(4 * g, 4 * g + 4), slice(t * P, (t + 1) * P))
                    dve.tensor_tensor(xTl[at], ps_j[g][:, :].rearrange("p (k t) -> p k t", k=4),
                                      xTh[at].bitcast(F32), ALU.subtract).then_inc(j_lo, 1)

            def p_lo(h, g, b):
                o, n = PT_GROUP[g]
                dve.wait_ge(t_hi, 3 * (8 * b + h) + g + 1)
                dve.tensor_tensor(PTl[:, o:o + n], ps_t[g % 2][:, 0:n], PTh[:, o:o + n].bitcast(F32),
                                  ALU.subtract).then_inc(t_lo, 1)

            def q_lo(p, b):
                bank = j_bank(("q", p))
                dve.wait_ge(j_hi, j_index(("q", p), b) + 1)
                for s in range(2):
                    own, other = (slice(0, HD), slice(HD, P)) if s == 0 else (slice(HD, P), slice(0, HD))
                    last = dve.scalar_tensor_tensor(
                        out=qst[other, p % 2, s, :], in0=ps_j[bank][own, :], scalar=bqk_s[own, p:p + 1],
                        in1=qst[own, p % 2, s, :].bitcast(F32), op0=ALU.add, op1=ALU.subtract)
                last.then_inc(j_lo, 1)

            def k_lo(p, b):
                bank = j_bank(("k", p))
                dve.wait_ge(j_hi, j_index(("k", p), b) + 1)
                for s in range(2):
                    own = slice(0, HD) if s == 0 else slice(HD, P)
                    last = dve.scalar_tensor_tensor(
                        out=kst[own, p % 2, s, 1, :], in0=ps_j[bank][own, :],
                        scalar=bqk_s[own, NPAIR + p:NPAIR + p + 1],
                        in1=kst[own, p % 2, s, 0, :].bitcast(F32), op0=ALU.add, op1=ALU.subtract)
                last.then_inc(j_lo, 1)

            def v_lo(t, b):
                bank = j_bank(("v", t))
                dve.wait_ge(j_hi, j_index(("v", t), b) + 1)
                dve.tensor_tensor(v[:, t, :, HD:2 * HD], ps_j[bank][:, :].rearrange("p (h c) -> p h c", h=NH),
                                  v[:, t, :, 0:HD].bitcast(F32), ALU.subtract).then_inc(j_lo, 1)

            def scores_max(h, b):
                H, q = 8 * b + h, h % 2
                dve.wait_ge(held, 1 + H)
                dve.wait_ge(s_done, H + 1)
                dve.memset(hold[:, 0:1], 0.0).then_inc(held, 1)
                m = maskf[:, :].bitcast(U32)
                diag = ps_s[:, 384:1536].rearrange("p (i c) -> p i c", c=384)[:, :, 0:P]
                dve.copy_predicated(diag, m.unsqueeze(1).to_broadcast([P, 3, P]),
                                    masked[:, :].unsqueeze(1).to_broadcast([P, 3, P])).then_inc(mask_done, 1)
                dve.copy_predicated(ps_s[:, 896:1024], m, masked[:, :].to_broadcast([P, P])).then_inc(mask_done, 1)
                dve.wait_ge(mask_done, 2 * H + 2)
                for i in range(NT):
                    last = dve.tensor_reduce(nm[:, q, i:i + 1], ps_s[:, S_OFF[i]:S_OFF[i] + (i + 1) * P],
                                             AX.X, ALU.max, negate=True)
                last.then_inc(max_done, 1)
                dve.wait_ge(max_done, H + 1)
                dve.tensor_scalar(nm[:, q, 0:3], nm[:, q, 0:3], -MASKED, None, ALU.min).then_inc(nm_ready, 1)

            def reciprocal(h, b):
                dve.wait_ge(den_ready, 8 * b + h + 1)
                dve.reciprocal(rden[:, h % 2, :], den[:, h % 2, :]).then_inc(rden_ready, 1)

            def vals_sum(h, b):
                H = 8 * b + h
                dve.wait_ge(vlo_done, H + 1)
                dve.wait_ge(vals_stored, 16 + 16 * H)
                dve.scalar_tensor_tensor(out=vt[0:HD, :], in0=ps_v[0:HD, :], scalar=bv_s[:, h:h + 1],
                                         in1=vt[HD:P, :], op0=ALU.add, op1=ALU.add).then_inc(vals_ready, 1)

            def lows(h, part, b, last):
                for kind, p, row, ks in between(h, part, b, last):
                    if ks is not FIRST:
                        {"q": q_lo, "k": k_lo, "v": v_lo, "x": x_lo}[kind](p, row)

            def body(b, last):
                for h in range(SLOTS):
                    if h < NH:
                        scores_max(h, b)
                    lows(h, 0, b, last)
                    if h == 5 and not last:
                        layernorm_stats(3, b + 1)
                    if h >= 2:
                        vals_sum(h - 2, b)
                    if 1 <= h <= NH:
                        for g in range(2):
                            p_lo(h - 1, g, b)
                    if h < NH:
                        reciprocal(h, b)
                    lows(h, 1, b, last)
                    if 1 <= h <= NH:
                        p_lo(h - 1, 2, b)
                    if not last:
                        if h < 3:
                            layernorm_stats(h, b + 1)

            def split_w(k):
                dve.wait_ge(w_hi, k + 1)
                dve.tensor_tensor(wl[:, k, :], raw[:, k % 4, :], wh[:, k, :].bitcast(F32), ALU.subtract)\
                    .then_inc(w_ready, 1)

            for t in range(3):
                layernorm_stats(t, 0)
            for t in range(3):
                x_lo(t, 0)
            for k in range(2):
                split_w(k)
            layernorm_stats(3, 0)
            for k in range(2, 4):
                split_w(k)
            x_lo(3, 0)
            for k in range(4, KD):
                split_w(k)
            dve.wait_ge(bias_landed, 32)
            dve.wait_ge(consts, 14)
            for p in range(2):
                k_lo(p, 0)
                q_lo(p, 0)
            with dve.Fori(0, NB - 1) as b:
                body(b, False)
            body(NB - 1, True)

        @block.scalar
        def _(act):
            def x_hi(t, b):
                for g in range(2):
                    act.wait_ge(j_full[g], j_uses(("x", t, g), b))
                    act.activation(xTh[:, 4 * g:4 * g + 4, t * P:(t + 1) * P],
                                   ps_j[g][:, :].rearrange("p (k t) -> p k t", k=4), ACT.Copy).then_inc(j_hi, 1)

            def p_hi(h, g, b):
                o, n = PT_GROUP[g]
                act.wait_ge(t_full[g % 2], 2 * (8 * b + h) + g // 2 + 1)
                act.activation(PTh[:, o:o + n], ps_t[g % 2][:, 0:n], ACT.Copy).then_inc(t_hi, 1)

            def masked_spread(h, b):
                act.wait_ge(t_full[1], 2 * (8 * b + h) + 2)
                act.activation(WT[:, :], ps_t[1][:, 0:3 * P], ACT.Copy).then_inc(wt_ready, 1)

            def q_hi(p, b):
                bank = j_bank(("q", p))
                act.wait_ge(j_full[bank], j_uses(("q", p), b))
                for s in range(2):
                    own = slice(0, HD) if s == 0 else slice(HD, P)
                    last = act.activation(qst[own, p % 2, s, :], ps_j[bank][own, :], ACT.Identity,
                                          bias=bqk_s[own, p:p + 1])
                last.then_inc(j_hi, 1)

            def k_hi(p, b):
                bank = j_bank(("k", p))
                act.wait_ge(j_full[bank], j_uses(("k", p), b))
                for s in range(2):
                    own = slice(0, HD) if s == 0 else slice(HD, P)
                    last = act.activation(kst[own, p % 2, s, 0, :], ps_j[bank][own, :], ACT.Identity,
                                          bias=bqk_s[own, NPAIR + p:NPAIR + p + 1])
                last.then_inc(j_hi, 1)

            def v_hi(t, b):
                bank = j_bank(("v", t))
                act.wait_ge(j_full[bank], j_uses(("v", t), b))
                act.activation(v[:, t, :, 0:HD], ps_j[bank][:, :].rearrange("p (h c) -> p h c", h=NH), ACT.Copy)\
                    .then_inc(j_hi, 1)

            def exps(h, b):
                H, q = 8 * b + h, h % 2
                act.wait_ge(nm_ready, H + 1)
                act.activation(wm[:, q, 0:3], nm[:, q, 0:3], ACT.Exp, bias=masked[:, :])
                for i in range(NT):
                    n = (i + 1) * P
                    last = act.activation(pr[:, q, S_OFF[i]:S_OFF[i] + n], ps_s[:, S_OFF[i]:S_OFF[i] + n], ACT.Exp,
                                          bias=nm[:, q, i:i + 1], accum_out=acc[:, q, i:i + 1])
                last.then_inc(exp_done, 1)

            def vals_lo_part(h, b):
                H = 8 * b + h
                act.wait_ge(pv_done, H + 1)
                act.wait_ge(vals_ready, 1 + H)
                act.activation(vt[HD:P, :], ps_v[HD:P, :], ACT.Copy).then_inc(vlo_done, 1)

            def highs(h, part, b, last, kinds="qkvx"):
                for kind, p, row, ks in between(h, part, b, last):
                    if ks is not FIRST and kind in kinds:
                        {"q": q_hi, "k": k_hi, "v": v_hi, "x": x_hi}[kind](p, row)

            def body(b, last):
                for h in range(SLOTS):
                    highs(h, 0, b, last, "x")
                    if h < NH:
                        exps(h, b)
                    highs(h, 0, b, last, "qkv")
                    if h >= 2:
                        vals_lo_part(h - 2, b)
                    if 1 <= h <= NH:
                        for g in range(2):
                            p_hi(h - 1, g, b)
                    highs(h, 1, b, last)
                    if 1 <= h <= NH:
                        p_hi(h - 1, 2, b)
                        masked_spread(h - 1, b)

            def split_w(k):
                act.wait_ge(w_landed[k % 4], 16 * (k // 4 + 1))
                act.activation(wh[:, k, :], raw[:, k % 4, :], ACT.Copy).then_inc(w_hi, 1)

            for t in range(3):
                x_hi(t, 0)
            for k in range(4):
                split_w(k)
            x_hi(3, 0)
            for k in range(4, KD):
                split_w(k)
            act.wait_ge(bias_landed, 32)
            act.wait_ge(consts, 14)
            for p in range(2):
                k_hi(p, 0)
                q_hi(p, 0)
            with act.Fori(0, NB - 1) as b:
                body(b, False)
            body(NB - 1, True)

        @block.tensor
        def _(pe):
            def bank_free(entry, b):
                n = j_index(entry, b)
                if not (isinstance(n, int) and n < 2):
                    pe.wait_ge(j_lo, n - 1)

            def transpose_x(t, b):
                pe.wait_ge(xn_ready, 4 * b + t + 1)
                for g in range(2):
                    bank_free(("x", t, g), b)
                    for k in range(4):
                        last = pe.transpose(ps_j[g][:, k * P:(k + 1) * P],
                                            xs[:, x_slot(t), (4 * g + k) * P:(4 * g + k + 1) * P], ident[:, :])
                    last.then_inc(j_full[g], 1)

            def project(kind, p, b, ks):
                bank = j_bank((kind, p))
                if 0 in ks:
                    bank_free((kind, p), b)
                c = (kind == "k") * PART + p * P
                for k in ks:
                    if (kind, p) == ("k", 0) and k in (0, 4):
                        pe.wait_ge(j_lo, j_index(("x", 3, k // 4), b) + 1)
                    if (kind, p) == ("k", 0) and isinstance(b, int) and b == 0:
                        pe.wait_ge(w_ready, k + 1)
                    for w, xT in ((wh, xTh), (wh, xTl), (wl, xTh)):
                        last = pe.matmul(ps_j[bank][:, :], w[:, k, c:c + P], xT[:, k, :],
                                         start=(k == 0 and w is wh and xT is xTh), stop=(k == KD - 1 and w is wl),
                                         skip_group_check=True)
                if KD - 1 in ks:
                    last.then_inc(j_full[bank], 1)

            def project_v(t, b):
                bank = j_bank(("v", t))
                bank_free(("v", t), b)
                for k in range(KD):
                    for xT, w in ((xTh, wh), (xTh, wl), (xTl, wh)):
                        last = pe.matmul(ps_j[bank][:, :], xT[:, k, t * P:(t + 1) * P], w[:, k, 2 * PART:3 * PART],
                                         start=(k == 0 and xT is xTh and w is wh), stop=(k == KD - 1 and xT is xTl))
                last.then_inc(j_full[bank], 1)

            def scores(h, b):
                H, p, s = 8 * b + h, h // 2, h % 2
                if h % 2 == 0:
                    pe.wait_ge(j_lo, j_index(("q", p), b) + 1)
                    pe.wait_ge(k_dup[p % 2], 32 * (2 * b + p // 2 + 1))
                if h > 0:
                    pe.wait_ge(exp_done, H)
                for i in range(NT):
                    for part in range(2):
                        last = pe.matmul(ps_s[:, S_OFF[i]:S_OFF[i] + (i + 1) * P],
                                         qst[:, p % 2, s, i * P:(i + 1) * P],
                                         kst[:, p % 2, s, part, 0:(i + 1) * P],
                                         start=(part == 0), stop=(part == 1), skip_group_check=True)
                last.then_inc(s_done, 1)

            def transpose_p(h, g, b):
                bank, H = g % 2, 8 * b + h
                if g >= 2:
                    pe.wait_ge(t_lo, 3 * H + g - 1)
                elif g == 0 and h > 0:
                    pe.wait_ge(t_lo, 3 * H)
                elif g == 1 and h > 0:
                    pe.wait_ge(wt_ready, H)
                if g == 0:
                    pe.wait_ge(p_ready, H + 1)
                if g == 3:
                    pe.wait_ge(d_ready, H + 1)
                    pe.matmul(ps_t[bank][:, 0:3 * P], ones[:, :], Dw[:, :], start=True, stop=True)\
                        .then_inc(t_full[bank], 1)
                    return
                o, n = PT_GROUP[g]
                for i, j, at in PT_BLOCKS:
                    if o <= at < o + n:
                        last = pe.transpose(ps_t[bank][:, at - o:at - o + P],
                                            pr[:, h % 2, S_OFF[i] + j * P:S_OFF[i] + (j + 1) * P], ident[:, :])
                last.then_inc(t_full[bank], 1)

            def values(h, b):
                H = 8 * b + h
                pe.wait_ge(t_lo, 3 * H + 3)
                if h == 0:
                    pe.wait_ge(j_lo, j_index(("v", 3), b) + 1)
                pe.wait_ge(wt_ready, H + 1)
                pe.wait_ge(vals_ready, 1 + H)
                for j in range(NT):
                    n = (NT - j) * P
                    for PT in (PTh, PTl):
                        pe.matmul(ps_v[:, j * P:], v[:, j, h, :], PT[:, PT_OFF[j]:PT_OFF[j] + n],
                                  start=(j == 0 and PT is PTh), stop=False, skip_group_check=True)
                    if j > 0:
                        last = pe.matmul(ps_v[:, 0:j * P], v[:, j, h, :], WT[:, 0:j * P],
                                         start=False, stop=(j == NT - 1), skip_group_check=True)
                last.then_inc(pv_done, 1)

            def step(kind, p, b, ks):
                if kind == "x":
                    transpose_x(p, b)
                elif kind == "v":
                    project_v(p, b)
                else:
                    project(kind, p, b, ks)

            def body(b, last):
                for h in range(SLOTS):
                    if h < NH:
                        scores(h, b)
                    for args in between(h, 0, b, last):
                        step(*args)
                    if h >= 2:
                        values(h - 2, b)
                    if 1 <= h <= NH:
                        transpose_p(h - 1, 0, b)
                        transpose_p(h - 1, 1, b)
                    for args in between(h, 1, b, last):
                        step(*args)
                    if 1 <= h <= NH:
                        transpose_p(h - 1, 2, b)
                        transpose_p(h - 1, 3, b)

            pe.wait_ge(consts, 14)
            for t in range(NT):
                transpose_x(t, 0)
            for p in range(2):
                project("k", p, 0, WHOLE)
                project("q", p, 0, WHOLE)
            with pe.Fori(0, NB - 1) as b:
                body(b, False)
            body(NB - 1, True)


def output_phase(nc, x, valsT, woT, bo, wagT, bf, gb, BT, out):
    NB, S, D = x.shape
    PART = woT.shape[0]
    R = BT.shape[0]
    RANKS = (8, 16, 32, 64)
    NG = len(RANKS)
    NAG = wagT.shape[1]
    GW = NAG // 3
    assert 3 * GW == NAG and GW <= 512 and 2 * GW < D
    U0 = D - 2 * GW
    G0 = U0 + R
    BANK_COLS = [(0, GW), (GW, 2 * GW), (2 * GW, D)]
    BANK_ORDER = (2, 0, 1)
    KD = D // P
    KV = PART // P
    H = 512

    with ExitStack() as ctx:
        def sb(name, shape, dt, c=ctx):
            return c.enter_context(nc.sbuf_tensor(name, shape, dt))

        def sem(name):
            return ctx.enter_context(nc.semaphore(name))

        wagh = sb("wagh", [P, KD, NAG], F32R)
        wagl = sb("wagl", [P, KD, NAG], F32R)
        woh = sb("woh", [P, KV, D], F32R)
        wol = sb("wol", [P, KV, D], F32R)
        Bh = sb("Bh", [P, D], F32R)
        Bl = sb("Bl", [P, D], F32R)
        vraw = sb("vraw", [P, 2, KV, P], F32)
        vh = sb("vh", [P, 2, KV, P], F32R)
        vl = sb("vl", [P, 2, KV, P], F32R)
        xs = sb("xt", [P, 2, D], F32)
        y = sb("y", [P, D], F32)
        z = sb("z", [P, D], F32)
        x1 = sb("x1", [P, 2, D], F32)
        x2n = sb("x2n", [P, D], F32)
        x2Th = sb("x2Th", [P, KD, P], F32R)
        x2Tl = sb("x2Tl", [P, KD, P], F32R)
        bo_s = sb("bo_s", [P, D], F32)
        bf_s = sb("bf_s", [P, D], F32)
        gb_s = sb("gb_s", [P, NG], F32)
        ident = sb("ident2", [P, P], F32)
        scores = sb("scores", [P, NG], F32)
        pmax = sb("pmax", [P, 2], F32)
        tmax = sb("tmax", [P, 2], F32)
        keep = sb("keep", [P, NG], F32)
        um = sb("um", [P, R], F32)
        us = sb("us", [P, 2 * R], F32)
        uT = sb("uT", [P, P], F32R)
        stats = sb("stats2", [P, 3, 12], F32)
        mv = sb("mv2", [P, 3, 2], F32)
        var_eps = sb("var_eps2", [P, 3], F32)
        rstd = sb("rstd2", [P, 3], F32)
        shift = sb("shift", [P, 3], F32)
        mhalf = sb("mhalf2", [P, 1], F32)
        eps = sb("eps2", [P, 1], F32)
        hold = sb("hold2", [1, 8], F32)
        with ExitStack() as early:
            raw = sb("raw2", [P, 4, NAG], F32, early)
        f = sb("f", [P, D], F32)
        zf = sb("zf", [P, D], F32)
        outs = sb("outs", [P, 2, D], F32)

        ps_f = ctx.enter_context(nc.psum_tensor("ps_f", [P, 3, 512], F32))
        ps_o = ctx.enter_context(nc.psum_tensor("ps_o", [P, 2, 512], F32))
        ps_x = ctx.enter_context(nc.psum_tensor("ps_x", [P, 2, 512], F32))
        ps_u = ctx.enter_context(nc.psum_tensor("ps_u", [P, 512], F32))

        bias_landed = sem("bias2_landed")
        w_landed = [sem(f"w2_landed{i}") for i in range(4)]
        w_hi = sem("w2_hi")
        w_ready = sem("w2_ready")
        v_landed = [sem(f"v_landed{i}") for i in range(2)]
        x_landed = [sem(f"xt_landed{i}") for i in range(2)]
        consts = sem("consts2")
        v_hi = sem("v_hi")
        v_ready = sem("v_ready")
        o_full = sem("o_full")
        y_done = sem("y_done")
        mv_ready = [sem(f"mv_ready{i}") for i in range(3)]
        ln_ready = [sem(f"ln_ready{i}") for i in range(3)]
        z_done = sem("z_done")
        x1_done = sem("x1_done")
        x2n_ready = sem("x2n_ready")
        x2_full = sem("x2_full")
        x2_hi = sem("x2_hi")
        x2_lo = sem("x2_lo")
        u_full = sem("u_full")
        us_ready = sem("us_ready")
        ut_full = sem("ut_full")
        ut_ready = sem("ut_ready")
        f_full = sem("f_full")
        f_done = sem("f_done")
        zf_done = sem("zf_done")
        out_done = sem("out_done")
        out_stored = [sem(f"out_stored{i}") for i in range(2)]

        CHUNKS = [("wo", k) for k in range(KV)] + [("B", 0)] + [("wag", k) for k in range(KD)]
        xf = x.rearrange("b s d -> (b s) d")
        outf = out.rearrange("b s d -> (b s) d")

        def vals_tile(b, i):
            b, i = b + i // 4, i % 4
            return valsT.rearrange("b (k p) t -> b p k t", p=P)[bass.ds(b, 1), :, :, i * P:(i + 1) * P]\
                .rearrange("b p k t -> (b p) k t")

        block = ctx.enter_context(nc.Block())

        @block.sync
        def _(sp):
            def load_v(b, i):
                sp.dma_start(vraw[:, i % 2, :, :], vals_tile(b, i)).then_inc(v_landed[i % 2], 16)

            def load_x(b, i):
                sp.dma_start(xs[:, i % 2, :], xf[bass.ds(b * S + i * P, P), :]).then_inc(x_landed[i % 2], 16)

            def body(b, last):
                for i in range(4):
                    if not (last and i + 2 > 3):
                        sp.wait_ge(x1_done, 2 * (4 * b + i) + 4)
                        load_x(b, i + 2)
                    if not (last and i + 3 > 3):
                        sp.wait_ge(v_ready, 4 * b + i + 2)
                        load_v(b, i + 3)
                    sp.wait_ge(out_done, 1 + 4 * b + i + 1)
                    sp.dma_start(outf[bass.ds(b * S + i * P, P), :], outs[:, i % 2, :]).then_inc(out_stored[i % 2], 16)

            sp.dma_start(bo_s[:, :], bo.partition_broadcast(P)).then_inc(bias_landed, 16)
            for n, (what, k) in enumerate(CHUNKS):
                if n >= 4:
                    sp.wait_ge(w_ready, n - 3)
                if what == "wo":
                    sp.dma_start(raw[:, n % 4, 0:D], woT[k * P:(k + 1) * P, :]).then_inc(w_landed[n % 4], 16)
                elif what == "wag":
                    sp.dma_start(raw[:, n % 4, :], wagT[k * P:(k + 1) * P, :]).then_inc(w_landed[n % 4], 16)
                else:
                    for half in range(2):
                        sp.dma_start(raw[half * R:(half + 1) * R, n % 4, 0:D], BT[:, :]).then_inc(w_landed[n % 4], 8 * 2)
                if n == 0:
                    load_v(0, 0)
                    load_v(0, 1)
                if n == 3:
                    load_x(0, 0)
                    load_x(0, 1)
                    sp.dma_start(bf_s[:, :], bf.partition_broadcast(P)).then_inc(bias_landed, 16)
                    sp.dma_start(gb_s[:, :], gb.partition_broadcast(P)).then_inc(bias_landed, 16)
            sp.wait_ge(v_ready, 1)
            load_v(0, 2)
            with sp.Fori(0, NB - 1) as b:
                body(b, False)
            body(NB - 1, True)
            for q in range(2):
                sp.wait_ge(out_stored[q], 16 + 16 * 2 * NB)

        @block.gpsimd
        def _(pool):
            def layernorm_scale(c, n):
                pool.wait_ge(mv_ready[c], n + 1)
                pool.tensor_tensor(var_eps[:, c:c + 1], mv[:, c, 1:2], eps[:, :], ALU.add)
                pool.drain()
                pool.tensor_tensor(rstd[:, c:c + 1], var_eps[:, c:c + 1], mhalf[:, :], ALU.pow)
                pool.drain()
                pool.tensor_scalar(shift[:, c:c + 1], mv[:, c, 0:1], rstd[:, c:c + 1], -1.0, ALU.mult, ALU.mult)\
                    .then_inc(ln_ready[c], 1)

            def first_residual(b, i):
                n = 4 * b + i
                pool.wait_ge(x_landed[i % 2], 16 * (2 * b + i // 2 + 1))
                for half in range(2):
                    pool.wait_ge(z_done, 2 * n + half + 1)
                    cols = slice(H * half, H * half + H)
                    pool.tensor_tensor(x1[:, i % 2, cols], xs[:, i % 2, cols], z[:, cols], ALU.add).then_inc(x1_done, 1)

            def second_residual(b, i):
                n = 4 * b + i
                pool.wait_ge(out_stored[i % 2], 16 + 16 * (2 * b + i // 2))
                pool.wait_ge(zf_done, 1 + n + 1)
                pool.tensor_tensor(outs[:, i % 2, :], x1[:, i % 2, :], zf[:, :], ALU.add).then_inc(out_done, 1)

            def body(b, last):
                for i in range(4):
                    if not (last and i == 3):
                        layernorm_scale(0, 4 * b + i + 1)
                        first_residual(b, i + 1)
                        layernorm_scale(1, 4 * b + i + 1)
                    layernorm_scale(2, 4 * b + i)
                    second_residual(b, i)

            pool.memset(ident[:, :], 0.0).then_inc(consts, 1)
            pool.memset(mhalf[:, :], -0.5).then_inc(consts, 1)
            pool.memset(eps[:, :], EPS).then_inc(consts, 1)
            pool.memset(keep[:, :], 1.0).then_inc(consts, 1)
            starts = ((zf_done, 1), (out_done, 1), (x2_full, 2), (x1_done, 2), (out_stored[0], 16),
                      (out_stored[1], 16), (f_done, 3))
            for at, (done, turn) in enumerate(starts):
                pool.memset(hold[:, at:at + 1], 0.0).then_inc(done, turn)
            pool.wait_ge(consts, 4)
            pool.affine_select(out=ident[:, :], in_=ident[:, :], compare_op=ALU.not_equal, fill=1.0, base=0,
                               pattern=[[-1, P]], channel_multiplier=1).then_inc(consts, 1)
            layernorm_scale(0, 0)
            first_residual(0, 0)
            layernorm_scale(1, 0)
            with pool.Fori(0, NB - 1) as b:
                body(b, False)
            body(NB - 1, True)

        @block.vector
        def _(dve):
            def half_statistics(c, t, i):
                dve.bn_stats(stats[:, c, 6 * i:6 * i + 6], t[:, H * i:H * i + H])

            def mean_and_variance(c):
                dve.drain()
                dve.bn_aggr(mv[:, c, :], stats[:, c, :]).then_inc(mv_ready[c], 1)

            def attention_out(n):
                if not (isinstance(n, int) and n == 0):
                    dve.wait_ge(z_done, 2 * n)
                for half in range(2):
                    dve.wait_ge(o_full, 2 * n + half + 1)
                    dve.tensor_tensor(y[:, H * half:H * half + H], ps_o[:, half, :], bo_s[:, H * half:H * half + H],
                                      ALU.add).then_inc(y_done, 1)
                    dve.drain()
                    half_statistics(0, y, half)
                mean_and_variance(0)

            def route(n):
                dve.wait_ge(u_full, n + 1)
                dve.tensor_tensor(scores[:, :], ps_f[:, 2, G0:G0 + NG], gb_s[:, :], ALU.add)
                dve.drain()
                pairs = scores[:, :].rearrange("p (a c) -> p c a", c=2)
                dve.tensor_tensor(pmax[:, :], pairs[:, 0, :], pairs[:, 1, :], ALU.max)
                dve.drain()
                dve.tensor_tensor(tmax[:, 0:1], pmax[:, 1:2], scores[:, 1:2], ALU.max)
                dve.tensor_tensor(tmax[:, 1:2], pmax[:, 0:1], scores[:, 2:3], ALU.max)
                dve.drain()
                dve.tensor_tensor(keep[:, 1:2], tmax[:, 0:1], scores[:, 0:1], ALU.is_gt)
                dve.tensor_tensor(keep[:, 2:3], pmax[:, 1:2], pmax[:, 0:1], ALU.is_gt)
                dve.tensor_tensor(keep[:, 3:4], scores[:, 3:4], tmax[:, 1:2], ALU.is_gt)
                dve.drain()
                for r, (lo, hi) in enumerate(zip((0,) + RANKS, RANKS)):
                    dve.tensor_scalar(um[:, lo:hi], ps_f[:, 2, U0 + lo:U0 + hi], keep[:, r:r + 1], None, ALU.mult)
                dve.drain()
                dve.tensor_copy(us[:, 0:R].bitcast(F32R), um[:, :])
                dve.drain()
                dve.tensor_tensor(us[:, R:2 * R].bitcast(F32R), um[:, :], us[:, 0:R], ALU.subtract)\
                    .then_inc(us_ready, 1)

            def second_layernorm(b, i):
                for half in range(2):
                    dve.wait_ge(x1_done, 2 * (4 * b + i) + 2 + half + 1)
                    half_statistics(1, x1[:, i % 2, :], half)
                mean_and_variance(1)

            def x2_low(n):
                for g in range(2):
                    dve.wait_ge(x2_hi, 2 * n + g + 1)
                    dve.tensor_tensor(x2Tl[:, 4 * g:4 * g + 4, :],
                                      ps_x[:, g, :].rearrange("p (k t) -> p k t", k=4),
                                      x2Th[:, 4 * g:4 * g + 4, :].bitcast(F32), ALU.subtract).then_inc(x2_lo, 1)

            def v_low(b, i):
                dve.wait_ge(v_hi, 4 * b + i + 1)
                dve.tensor_tensor(vl[:, i % 2, :, :], vraw[:, i % 2, :, :], vh[:, i % 2, :, :].bitcast(F32),
                                  ALU.subtract).then_inc(v_ready, 1)

            def ffn_out(n):
                dve.wait_ge(zf_done, 1 + n)
                for m, g in enumerate(BANK_ORDER):
                    lo, hi = BANK_COLS[g]
                    dve.wait_ge(f_full, 3 * n + m + 1)
                    dve.tensor_tensor(f[:, lo:hi], ps_f[:, g, 0:hi - lo], bf_s[:, lo:hi], ALU.add).then_inc(f_done, 1)
                dve.drain()
                for half in range(2):
                    half_statistics(2, f, half)
                mean_and_variance(2)

            def body(b, last):
                for i in range(4):
                    n, more = 4 * b + i, not (last and i == 3)
                    if more:
                        attention_out(n + 1)
                    route(n)
                    if not (last and i + 2 > 3):
                        v_low(b, i + 2)
                    if more:
                        second_layernorm(b, i + 1)
                        x2_low(n + 1)
                    ffn_out(n)

            def split_w(n):
                what, k = CHUNKS[n]
                dve.wait_ge(w_hi, n + 1)
                if what == "wo":
                    dve.tensor_tensor(wol[:, k, :], raw[:, n % 4, 0:D], woh[:, k, :].bitcast(F32), ALU.subtract)\
                        .then_inc(w_ready, 1)
                elif what == "wag":
                    dve.tensor_tensor(wagl[:, k, :], raw[:, n % 4, :], wagh[:, k, :].bitcast(F32), ALU.subtract)\
                        .then_inc(w_ready, 1)
                else:
                    dve.tensor_tensor(Bl[:, :], raw[:, n % 4, 0:D], Bh[:, :].bitcast(F32), ALU.subtract)\
                        .then_inc(w_ready, 1)

            for n in range(4):
                split_w(n)
            v_low(0, 0)
            v_low(0, 1)
            for n in range(4, 7):
                split_w(n)
            dve.wait_ge(bias_landed, 48)
            dve.wait_ge(consts, 5)
            attention_out(0)
            for n in range(7, 9):
                split_w(n)
            second_layernorm(0, 0)
            for n in range(9, len(CHUNKS)):
                split_w(n)
            x2_low(0)
            with dve.Fori(0, NB - 1) as b:
                body(b, False)
            body(NB - 1, True)

        @block.scalar
        def _(act):
            def scaled(out_, in_, c):
                return act.activation(out_, in_, ACT.Identity, scale=rstd[:, c:c + 1], bias=shift[:, c:c + 1])

            def first_norm(n):
                act.wait_ge(ln_ready[0], n + 1)
                for half in range(2):
                    act.wait_ge(x1_done, 2 * n + half + 1)
                    cols = slice(H * half, H * half + H)
                    scaled(z[:, cols], y[:, cols], 0).then_inc(z_done, 1)

            def second_norm(b, i):
                n = 4 * b + i
                act.wait_ge(x2_full, 2 + 2 * n)
                act.wait_ge(ln_ready[1], n + 1)
                for half in range(2):
                    cols = slice(H * half, H * half + H)
                    scaled(x2n[:, cols], x1[:, i % 2, cols], 1).then_inc(x2n_ready, 1)

            def x2_high(n):
                for g in range(2):
                    act.wait_ge(x2_full, 2 + 2 * n + g + 1)
                    act.activation(x2Th[:, 4 * g:4 * g + 4, :], ps_x[:, g, :].rearrange("p (k t) -> p k t", k=4),
                                   ACT.Copy).then_inc(x2_hi, 1)

            def v_high(b, i):
                act.wait_ge(v_landed[i % 2], 16 * (2 * b + i // 2 + 1))
                if not (isinstance(b, int) and 4 * b + i < 2):
                    act.wait_ge(o_full, 2 * (4 * b + i) - 2)
                act.activation(vh[:, i % 2, :, :], vraw[:, i % 2, :, :], ACT.Copy).then_inc(v_hi, 1)

            def u_transposed(n):
                act.wait_ge(ut_full, n + 1)
                act.activation(uT[:, :], ps_u[:, 0:P], ACT.Copy).then_inc(ut_ready, 1)

            def last_norm(n):
                act.wait_ge(out_done, 1 + n)
                act.wait_ge(ln_ready[2], n + 1)
                scaled(zf[:, :], f[:, :], 2).then_inc(zf_done, 1)

            def body(b, last):
                for i in range(4):
                    n, more = 4 * b + i, not (last and i == 3)
                    if not (last and i + 2 > 3):
                        v_high(b, i + 2)
                    if more:
                        first_norm(n + 1)
                    u_transposed(n)
                    if more:
                        second_norm(b, i + 1)
                        x2_high(n + 1)
                    last_norm(n)

            def split_w(n):
                what, k = CHUNKS[n]
                act.wait_ge(w_landed[n % 4], 16 * (n // 4 + 1) + (16 if n % 4 == 0 and n >= 4 else 0))
                if what == "wo":
                    act.activation(woh[:, k, :], raw[:, n % 4, 0:D], ACT.Copy).then_inc(w_hi, 1)
                elif what == "wag":
                    act.activation(wagh[:, k, :], raw[:, n % 4, :], ACT.Copy).then_inc(w_hi, 1)
                else:
                    act.activation(Bh[:, :], raw[:, n % 4, 0:D], ACT.Copy).then_inc(w_hi, 1)

            for n in range(4):
                split_w(n)
            v_high(0, 0)
            v_high(0, 1)
            for n in range(4, 9):
                split_w(n)
            first_norm(0)
            for n in range(9, len(CHUNKS)):
                split_w(n)
            second_norm(0, 0)
            x2_high(0)
            with act.Fori(0, NB - 1) as b:
                body(b, False)
            body(NB - 1, True)

        @block.tensor
        def _(pe):
            def attention_product(b, i):
                n = 4 * b + i
                pe.wait_ge(v_ready, n + 1)
                for half in range(2):
                    if not (isinstance(n, int) and n == 0):
                        pe.wait_ge(y_done, 2 * n - 1 + half)
                    cols = slice(H * half, H * half + H)
                    for k in range(KV):
                        for a, w in ((vh, woh), (vh, wol), (vl, woh)):
                            last = pe.matmul(ps_o[:, half, :], a[:, i % 2, k, :], w[:, k, cols],
                                             start=(k == 0 and a is vh and w is woh), stop=(k == KV - 1 and a is vl))
                    last.then_inc(o_full, 1)

            def transpose_x2(n):
                for g in range(2):
                    pe.wait_ge(x2n_ready, 2 * n + g + 1)
                    if not (isinstance(n, int) and n == 0):
                        pe.wait_ge(x2_lo, 2 * n - 1 + g)
                    for k in range(4):
                        last = pe.transpose(ps_x[:, g, k * P:(k + 1) * P], x2n[:, (4 * g + k) * P:(4 * g + k + 1) * P],
                                            ident[:, :])
                    last.then_inc(x2_full, 1)

            def ffn(n):
                pe.wait_ge(x2_lo, 2 * n + 2)
                pe.wait_ge(f_done, 3 + 3 * n)
                for g in BANK_ORDER:
                    cols = slice(GW * g, GW * g + GW)
                    for k in range(KD):
                        for a, w in ((x2Th, wagh), (x2Th, wagl), (x2Tl, wagh)):
                            last = pe.matmul(ps_f[:, g, 0:GW], a[:, k, :], w[:, k, cols],
                                             start=(k == 0 and a is x2Th and w is wagh), stop=False,
                                             skip_group_check=True)
                    if g == 2:
                        last.then_inc(u_full, 1)
                    if g == 0:
                        pe.wait_ge(us_ready, n + 1)
                        pe.transpose(ps_u[:, 0:P], us[:, :], ident[:, :]).then_inc(ut_full, 1)
                pe.wait_ge(ut_ready, n + 1)
                for g in BANK_ORDER:
                    lo, hi = BANK_COLS[g]
                    for Bp in (Bh, Bl):
                        last = pe.matmul(ps_f[:, g, 0:hi - lo], uT[:, :], Bp[:, lo:hi], start=False,
                                         stop=(Bp is Bl), skip_group_check=True)
                    last.then_inc(f_full, 1)

            def body(b, last):
                for i in range(4):
                    n, more = 4 * b + i, not (last and i == 3)
                    if more:
                        attention_product(b, i + 1)
                    ffn(n)
                    if more:
                        transpose_x2(n + 1)

            pe.wait_ge(consts, 5)
            pe.wait_ge(w_ready, KV)
            attention_product(0, 0)
            transpose_x2(0)
            pe.wait_ge(w_ready, len(CHUNKS))
            with pe.Fori(0, NB - 1) as b:
                body(b, False)
            body(NB - 1, True)


def kernel(L0_attn_x, L0_attn_w_qkv, L0_attn_b_qkv, L0_attn_w_o, L0_attn_b_o, L0_ffn_W, L0_ffn_b, L0_ffn_A,
           L0_ffn_B, L0_ffn_gate_w, L0_ffn_gate_b):
    import numpy as np
    import concourse.bacc as bacc
    from concourse.bass_utils import run_bass_kernel_spmd

    c = np.ascontiguousarray
    x = np.asarray(L0_attn_x)
    b_qkv = np.asarray(L0_attn_b_qkv)
    part = b_qkv.shape[0] // 3
    arrays = {
        "x": c(x),
        "wqkvT": c(np.asarray(L0_attn_w_qkv).T),
        "bqk": c(b_qkv[:2 * part].reshape(-1, P).T),
        "bv": c(b_qkv[2 * part:].reshape(-1, 64).T),
        "woT": c(np.asarray(L0_attn_w_o).T),
        "bo": c(L0_attn_b_o),
        "wagT": c(np.concatenate([np.asarray(L0_ffn_W).T, np.asarray(L0_ffn_A).T, np.asarray(L0_ffn_gate_w).T], axis=1)),
        "bf": c(L0_ffn_b),
        "gb": c(L0_ffn_gate_b),
        "BT": c(np.asarray(L0_ffn_B).T),
    }
    nc = bacc.Bacc("TRN2", target_bir_lowering=False, num_devices=1)
    aps = {k: nc.dram_tensor(f"in_{k}", a.shape, mybir.dt.from_np(a.dtype), kind="ExternalInput").ap()
           for k, a in arrays.items()}
    valsT = nc.dram_tensor("valsT", (x.shape[0], part, x.shape[1]), F32, kind="Internal").ap()
    out = nc.dram_tensor("out", x.shape, F32, kind="ExternalOutput").ap()
    attention_phase(nc, aps["x"], aps["wqkvT"], aps["bqk"], aps["bv"], valsT)
    output_phase(nc, aps["x"], valsT, aps["woT"], aps["bo"], aps["wagT"], aps["bf"], aps["gb"], aps["BT"], out)
    r = run_bass_kernel_spmd(nc, [{f"in_{k}": a for k, a in arrays.items()}], core_ids=[0])
    return r.results[0]["out"]
```

```python
from contextlib import ExitStack

import concourse.bass as bass
from concourse import mybir

ALU = mybir.AluOpType
ACT = mybir.ActivationFunctionType
AX = mybir.AxisListType
F32 = mybir.dt.float32
F32R = mybir.dt.float32r
U32 = mybir.dt.uint32

P = 128
EPS = 1e-5
MASKED = -10000.0


class OutputWeights:

    def __init__(self, nc, ctx, NB, S, D, PART, R, NAG):
        def sb(name, shape, dt, c=ctx):
            return c.enter_context(nc.sbuf_tensor(name, shape, dt))

        KD, KV = D // P, PART // P
        self.R, self.KV = R, KV
        self.SPLIT_EARLY = 7
        with ExitStack() as early:
            wag_raw = sb("wag_raw", [P, KD, NAG], F32, early)
            wo_raw = sb("wo_raw", [P, KV, D], F32, early)
            B_raw = sb("B_raw", [P, D], F32, early)
        self.wagl = sb("wagl", [P, KD, NAG], F32R)
        self.wol = sb("wol", [P, KV, D], F32R)
        self.Bl = sb("Bl", [P, D], F32R)
        self.wagh = sb("wagh", [P, KD, NAG], F32R)
        self.woh = sb("woh", [P, KV, D], F32R)
        self.Bh = sb("Bh", [P, D], F32R)
        self.vraw = sb("vraw", [P, 2, PART // P, P], F32)
        self.vh = sb("vh", [P, 2, PART // P, P], F32R)
        self.vl = sb("vl", [P, 2, PART // P, P], F32R)
        self.bo_s = sb("bo_s", [P, D], F32)
        self.xs = sb("xt", [P, 2, D], F32)
        self.floats = 2 * (D // P * NAG + PART // P * D + D) + 3 * 2 * PART + 3 * D
        self.chunks = [("wo", k, wo_raw[:, k, :], self.woh[:, k, :], self.wol[:, k, :]) for k in range(KV)]
        self.chunks += [("B", 0, B_raw[:, :], self.Bh[:, :], self.Bl[:, :])]
        self.chunks += [("wag", k, wag_raw[:, k, :], self.wagh[:, k, :], self.wagl[:, k, :]) for k in range(KD)]


def vals_tile(valsT, b, i):
    b, i = b + i // 4, i % 4
    return valsT.rearrange("b (k p) t -> b p k t", p=P)[bass.ds(b, 1), :, :, i * P:(i + 1) * P]\
        .rearrange("b p k t -> (b p) k t")


def attention_phase(nc, x, wqkvT, bqk, bv, valsT, vals_stored, ps_o, W, woT, bo, wagT, BT):
    NB, S, D = x.shape
    E = wqkvT.shape[1]
    PART = E // 3
    HD = 64
    NH = PART // HD
    NPAIR = NH // 2
    KD = D // P
    NT = S // P
    assert NT == 4 and NH == 8 and S == 512

    PT_OFF = [0, 512, 896, 1152]
    PT_N = 1280
    PT_GROUP = [(0, 512), (512, 512), (1024, 256)]
    PT_BLOCKS = [(i, j, PT_OFF[j] + (i - j) * P) for j in range(NT) for i in range(j, NT)]
    S_OFF = {3: 0, 2: 512, 0: 896, 1: 1024}

    WHOLE, FIRST, SECOND = range(KD), range(KD // 2), range(KD // 2, KD)
    BETWEEN = [
        ([("v", 0, 0, WHOLE), ("v", 1, 0, WHOLE)], []),
        ([("v", 2, 0, WHOLE)], [("v", 3, 0, WHOLE)]),
        ([("k", 2, 0, WHOLE)], [("q", 2, 0, FIRST)]),
        ([("q", 2, 0, SECOND)], [("k", 3, 0, WHOLE)]),
        ([("q", 3, 0, WHOLE)], [("x", 0, 1, WHOLE)]),
        ([("x", 1, 1, WHOLE)], [("x", 2, 1, WHOLE)]),
        ([("x", 3, 1, WHOLE)], [("k", 0, 1, WHOLE)]),
        ([("q", 0, 1, FIRST)], [("q", 0, 1, SECOND), ("k", 1, 1, FIRST)]),
        ([("k", 1, 1, SECOND)], [("q", 1, 1, FIRST)]),
        ([("q", 1, 1, SECOND)], []),
    ]
    BETWEEN_LAST = BETWEEN[:2] + [([(kind, p, 0, FIRST)], [(kind, p, 0, SECOND)])
                                  for kind, p in (("k", 2), ("q", 2), ("k", 3), ("q", 3))] + 4 * [([], [])]
    BARE = 6
    SLOTS = len(BETWEEN)
    AHEAD = (3, 4, 5, 6)
    EARLY = [("x", t, g) for t in range(NT) for g in range(2)] + [("k", 0), ("q", 0), ("k", 1), ("q", 1)]
    NOW = [("v", 0), ("v", 1), ("v", 2), ("v", 3), ("k", 2), ("q", 2), ("k", 3), ("q", 3)]

    with ExitStack() as ctx:
        def sb(name, shape, dt, c=ctx):
            return c.enter_context(nc.sbuf_tensor(name, shape, dt))

        def sem(name):
            return ctx.enter_context(nc.semaphore(name))

        wh = sb("wh", [P, KD, E], F32R)
        wl = sb("wl", [P, KD, E], F32R)
        xTh = sb("xTh", [P, KD, S], F32R)
        xTl = sb("xTl", [P, KD, S], F32R)
        assert W.floats - D <= 2 * KD * (E + S) + 2 * S
        qst = sb("qst", [P, 2, 2, S], F32R)
        kst = sb("kst", [P, 2, 2, 2, S], F32R)
        RAW = 5
        with ExitStack() as early:
            raw = sb("raw", [P, RAW, 2 * PART], F32, early)
            x3 = sb("x3", [P, D], F32, early)
        v = sb("v", [P, NT, NH, 2 * HD], F32R)
        PTh = sb("PTh", [P, PT_N], F32R)
        PTl = sb("PTl", [P, PT_N], F32R)
        WT = sb("WT", [P, 3 * P], F32R)
        Dw = sb("Dw", [P, 3 * P], F32R)
        ones = sb("ones", [P, P], F32R)
        xs = sb("xs", [P, 3, D], F32)
        pr = sb("pr", [P, 2, PT_N], F32)
        vt = sb("vt", [P, S], F32)
        ident = sb("ident", [P, P], F32)
        maskf = sb("maskf", [P, P], F32)
        masked = sb("masked", [P, 1], F32)
        cnt = sb("cnt", [P, 4], F32)
        bqk_s = sb("bqk_s", [P, 2 * NPAIR], F32)
        bv_s = sb("bv_s", [HD, NH], F32)
        stats = sb("stats", [P, 2, 12], F32)
        mv = sb("mv", [P, 2, 2], F32)
        var_eps = sb("var_eps", [P, 2], F32)
        rstd = sb("rstd", [P, 2], F32)
        nmean = sb("nmean", [P, 2], F32)
        mhalf = sb("mhalf", [P, 1], F32)
        mone = sb("mone", [P, 1], F32)
        eps = sb("eps", [P, 1], F32)
        hold = sb("hold", [1, 3], F32)
        nm = sb("nm", [P, 2, 4], F32)
        acc = sb("acc", [P, 2, 4], F32)
        wm = sb("wm", [P, 2, 4], F32)
        cw = sb("cw", [P, 2, 4], F32)
        den = sb("den", [P, 2, 4], F32)
        rden = sb("rden", [P, 2, 4], F32)
        wn = sb("wn", [P, 2, 4], F32)

        ps_s = ctx.enter_context(nc.psum_tensor("ps_s", [P, 3 * 512], F32))
        ps_j = [ps_o[:, i, :] for i in range(2)]
        ps_t = [ctx.enter_context(nc.psum_tensor(f"ps_t{i}", [P, 512], F32)) for i in range(2)]
        ps_v = ctx.enter_context(nc.psum_tensor("ps_v", [P, 512], F32))

        x_landed = [sem(f"x_landed{i}") for i in range(NT)]
        w_landed = [sem(f"w_landed{i}") for i in range(RAW)]
        bias_landed = sem("bias_landed")
        consts = sem("consts")
        w_hi = sem("w_hi")
        w_ready = sem("w_ready")
        mv_ready = sem("mv_ready")
        ve_done = sem("ve_done")
        xn_ready = sem("xn_ready")
        t_full = [sem(f"t_full{i}") for i in range(2)]
        t_hi = sem("t_hi")
        t_lo = sem("t_lo")
        wt_ready = sem("wt_ready")
        j_full = [sem(f"j_full{i}") for i in range(2)]
        j_hi = sem("j_hi")
        j_lo = sem("j_lo")
        k_dup = [sem(f"k_dup{i}") for i in range(2)]
        s_done = sem("s_done")
        held = sem("held")
        mask_done = sem("mask_done")
        max_done = sem("max_done")
        nm_ready = sem("nm_ready")
        exp_done = sem("exp_done")
        cw_done = sem("cw_done")
        den_ready = sem("den_ready")
        rden_ready = sem("rden_ready")
        wn_done = sem("wn_done")
        p_ready = sem("p_ready")
        d_ready = sem("d_ready")
        pv_done = sem("pv_done")
        vlo_done = sem("vlo_done")
        vals_ready = sem("vals_ready")
        next_landed = [sem(f"next_landed{n}") for n in range(len(W.chunks))]
        next_hi = sem("next_hi")
        next_lo = sem("next_lo")
        tiles_landed = sem("tiles_landed")
        v_first_landed = sem("v_first_landed")
        v_first_hi = sem("v_first_hi")
        v_first_lo = sem("v_first_lo")

        LOADS = {5: range(0, 4), 6: range(4, 8), 7: range(8, 11), 8: range(11, 13)}
        SPLITS = {6: range(0, 2), 7: range(2, 4), 8: range(4, W.SPLIT_EARLY)}

        xf = x.rearrange("b s d -> (b s) d")
        vf = valsT.rearrange("b c t -> (b c) t")

        W_CHUNKS = [[k] for k in range(KD)] + [[k, k + 1] for k in range(0, KD, 2)]

        def w_chunk(n, t):
            ks = W_CHUNKS[n]
            return t[:, ks[0], 0:2 * PART] if len(ks) == 1 else t[:, ks[0]:ks[0] + 2, 2 * PART:3 * PART]

        def raw_chunk(n):
            return raw[:, n % RAW, :] if n < KD else raw[:, n % RAW, :].rearrange("p (k c) -> p k c", k=2)

        def x_tile(t, b):
            if t == 3 and isinstance(b, int) and b == 0:
                return x3
            return xs[:, t % 3, :]

        def x_bank(t, g, b):
            return (ps_t if isinstance(b, int) and b == 0 and t % 2 else ps_j)[g]

        def pair_bank(kind, p, b):
            return ps_t[0] if (kind, p) == ("k", 1) and isinstance(b, int) and b == 0 else ps_j[j_bank((kind, p))]


        def j_index(entry, b):
            if entry in EARLY:
                return 20 * b + EARLY.index(entry)
            return 20 * b + len(EARLY) + NOW.index(entry)

        def j_bank(entry):
            return j_index(entry, 0) % 2

        def j_uses(entry, b):
            return 10 * b + j_index(entry, 0) // 2 + 1

        def between(h, part, b, last):
            return [(kind, p, b + ahead, ks) for kind, p, ahead, ks in (BETWEEN_LAST if last else BETWEEN)[h][part]]

        block = ctx.enter_context(nc.Block())

        @block.sync
        def _(sp):
            def load_x(t, b):
                sp.dma_start(x_tile(t, b)[:, :], xf[bass.ds(b * S + t * P, P), :]).then_inc(x_landed[t], 16)

            def dup_k(p, b):
                sp.wait_ge(j_lo, j_index(("k", p), b) + 1)
                sp.dma_start(kst[HD:P, p % 2, 0, :, :].bitcast(F32), kst[0:HD, p % 2, 0, :, :].bitcast(F32)).then_inc(k_dup[p % 2], 16)
                sp.dma_start(kst[0:HD, p % 2, 1, :, :].bitcast(F32), kst[HD:P, p % 2, 1, :, :].bitcast(F32)).then_inc(k_dup[p % 2], 16)

            def store_vals(h, b):
                sp.wait_ge(vals_ready, 1 + 8 * b + h + 1)
                sp.dma_start(vf[bass.ds(b * PART + h * HD, HD), :], vt[0:HD, :]).then_inc(vals_stored, 16)

            def load_next(n):
                what, k, raw_place, _, _ = W.chunks[n]
                if what == "B":
                    for half in range(2):
                        sp.dma_start(raw_place[half * W.R:(half + 1) * W.R, :], BT[:, :]).then_inc(next_landed[n], 16)
                else:
                    source = woT if what == "wo" else wagT
                    sp.dma_start(raw_place, source[k * P:(k + 1) * P, :]).then_inc(next_landed[n], 16)

            def body(b, last):
                if not last:
                    sp.wait_ge(j_lo, j_index(("x", 3, 1), b) + 1)
                    for t in range(3):
                        load_x(t, b + 1)
                for h in range(SLOTS):
                    if h >= 2:
                        store_vals(h - 2, b)
                    if h in (2, 4):
                        dup_k(h // 2 + 1, b)
                    if h == 4 and not last:
                        sp.wait_ge(j_full[1], j_uses(("x", 0, 1), b + 1))
                        load_x(3, b + 1)
                    if h in (7, 8) and not last:
                        dup_k(h - 7, b + 1)
                    if last and h == 5:
                        sp.wait_ge(j_full[j_bank(("q", 3))], j_uses(("q", 3), b))
                        for t in range(2):
                            sp.dma_start(W.vraw[:, t, :, :], vals_tile(valsT, 0, t)).then_inc(v_first_landed, 16)
                    if last and h in LOADS:
                        for n in LOADS[h]:
                            load_next(n)
                    if last and h == 8:
                        sp.dma_start(W.xs[:, 0, :], xf[0:P, :]).then_inc(tiles_landed, 16)
                        sp.dma_start(W.bo_s[:, :], bo.partition_broadcast(P)).then_inc(tiles_landed, 16)

            def load_w(n):
                if n >= RAW:
                    sp.wait_ge(w_ready, n - RAW + 1)
                ks = W_CHUNKS[n]
                if len(ks) == 1:
                    source = wqkvT[ks[0] * P:(ks[0] + 1) * P, 0:2 * PART]
                else:
                    source = wqkvT[ks[0] * P:(ks[0] + 2) * P, 2 * PART:3 * PART].rearrange("(k p) c -> p k c", p=P)
                sp.dma_start(raw_chunk(n), source).then_inc(w_landed[n % RAW], 16)

            for t in range(3):
                load_x(t, 0)
            load_x(3, 0)
            for n in range(3):
                load_w(n)
            sp.dma_start(bqk_s[:, :], bqk).then_inc(bias_landed, 16)
            sp.dma_start(bv_s[:, :], bv).then_inc(bias_landed, 16)
            for n in range(3, len(W_CHUNKS)):
                load_w(n)
            dup_k(0, 0)
            dup_k(1, 0)
            with sp.Fori(0, NB - 1) as b:
                body(b, False)
            body(NB - 1, True)
            sp.wait_ge(tiles_landed, 2 * 16)
            for n in range(W.SPLIT_EARLY, len(W.chunks)):
                sp.wait_ge(next_landed[n], 16)

        @block.gpsimd
        def _(pool):
            def layernorm(t, b):
                n, q = 4 * b + t, t % 2
                pool.wait_ge(mv_ready, n + 1)
                pool.tensor_tensor(var_eps[:, q:q + 1], mv[:, q, 1:2], eps[:, :], ALU.add).then_inc(ve_done, 1)
                pool.tensor_tensor(nmean[:, q:q + 1], mv[:, q, 0:1], mone[:, :], ALU.mult)
                pool.wait_ge(ve_done, n + 1)
                pool.tensor_tensor(rstd[:, q:q + 1], var_eps[:, q:q + 1], mhalf[:, :], ALU.pow)
                pool.drain()
                at = x_tile(t, b)[:, :]
                pool.tensor_scalar(at, at, nmean[:, q:q + 1], rstd[:, q:q + 1], ALU.add, ALU.mult)\
                    .then_inc(xn_ready, 1)

            def normalise(h, b):
                H, q = 8 * b + h, h % 2
                pool.wait_ge(exp_done, H + 1)
                pool.tensor_tensor(cw[:, q, :], wm[:, q, :], cnt[:, :], ALU.mult).then_inc(cw_done, 1)
                pool.wait_ge(cw_done, H + 1)
                pool.tensor_tensor(den[:, q, :], cw[:, q, :], acc[:, q, :], ALU.add).then_inc(den_ready, 1)
                pool.wait_ge(rden_ready, H + 1)
                pool.tensor_tensor(wn[:, q, :], wm[:, q, :], rden[:, q, :], ALU.mult).then_inc(wn_done, 1)
                for i in range(NT):
                    at = pr[:, q, S_OFF[i]:S_OFF[i] + (i + 1) * P]
                    last = pool.tensor_scalar(at, at, rden[:, q, i:i + 1], 1.0, ALU.mult, ALU.mult)
                last.then_inc(p_ready, 1)
                pool.wait_ge(wn_done, H + 1)
                if h > 0:
                    pool.wait_ge(wt_ready, H)
                pool.tensor_tensor(Dw[:, :].rearrange("p (i t) -> p i t", i=3),
                                   ident[:, :].unsqueeze(1).to_broadcast([P, 3, P]),
                                   wn[:, q, 0:3].unsqueeze(2).to_broadcast([P, 3, P]), ALU.mult).then_inc(d_ready, 1)

            def body(b, last):
                for h in range(NH):
                    if h == 5 and not last:
                        layernorm(3, b + 1)
                    normalise(h, b)
                    if h < 3 and not last:
                        layernorm(h, b + 1)

            pool.memset(ident[:, :], 0.0).then_inc(consts, 1)
            pool.memset(maskf[:, :], 0.0).then_inc(consts, 1)
            pool.memset(mhalf[:, :], -0.5).then_inc(consts, 1)
            pool.memset(mone[:, :], -1.0).then_inc(consts, 1)
            pool.memset(eps[:, :], EPS).then_inc(consts, 1)
            pool.memset(masked[:, :], MASKED).then_inc(consts, 1)
            for i in range(NT):
                pool.memset(cnt[:, i:i + 1], float(S - (i + 1) * P)).then_inc(consts, 1)
            pool.memset(wm[:, :, :], 0.0).then_inc(consts, 1)
            pool.memset(ones[:, :].bitcast(F32), 1.0).then_inc(consts, 1)
            pool.memset(hold[:, 1:2], 0.0).then_inc(vals_ready, 1)
            pool.memset(hold[:, 2:3], 0.0).then_inc(vals_stored, 16)
            pool.memset(hold[:, 0:1], 0.0).then_inc(held, 1)
            pool.wait_ge(consts, 12)
            pool.affine_select(out=ident[:, :], in_=ident[:, :], compare_op=ALU.not_equal, fill=1.0, base=0,
                               pattern=[[-1, P]], channel_multiplier=1).then_inc(consts, 1)
            pool.affine_select(out=maskf[:, :], in_=maskf[:, :], compare_op=ALU.is_ge, fill=1.0, base=0,
                               pattern=[[-1, P]], channel_multiplier=1).then_inc(consts, 1)
            for t in range(NT):
                layernorm(t, 0)
            with pool.Fori(0, NB - 1) as b:
                body(b, False)
            body(NB - 1, True)

        @block.vector
        def _(dve):
            def layernorm_stats(t, b):
                q, at = t % 2, x_tile(t, b)
                dve.wait_ge(x_landed[t], 16 * (b + 1))
                if not (isinstance(b, int) and 4 * b + t < 2):
                    dve.wait_ge(xn_ready, 4 * b + t - 1)
                for i in range(2):
                    dve.bn_stats(stats[:, q, 6 * i:6 * i + 6], at[:, 512 * i:512 * i + 512])
                dve.drain()
                dve.bn_aggr(mv[:, q, :], stats[:, q, :]).then_inc(mv_ready, 1)

            def x_lo(t, b):
                for g in range(2):
                    dve.wait_ge(j_hi, j_index(("x", t, g), b) + 1)
                    at = (slice(None), slice(4 * g, 4 * g + 4), slice(t * P, (t + 1) * P))
                    dve.tensor_tensor(xTl[at], x_bank(t, g, b)[:, :].rearrange("p (k t) -> p k t", k=4),
                                      xTh[at].bitcast(F32), ALU.subtract).then_inc(j_lo, 1)

            def p_lo(h, g, b):
                o, n = PT_GROUP[g]
                dve.wait_ge(t_hi, 3 * (8 * b + h) + g + 1)
                dve.tensor_tensor(PTl[:, o:o + n], ps_t[g % 2][:, 0:n], PTh[:, o:o + n].bitcast(F32),
                                  ALU.subtract).then_inc(t_lo, 1)

            def q_lo(p, b):
                ps = pair_bank("q", p, b)
                dve.wait_ge(j_hi, j_index(("q", p), b) + 1)
                for s in range(2):
                    own, other = (slice(0, HD), slice(HD, P)) if s == 0 else (slice(HD, P), slice(0, HD))
                    last = dve.scalar_tensor_tensor(
                        out=qst[other, p % 2, s, :], in0=ps[own, :], scalar=bqk_s[own, p:p + 1],
                        in1=qst[own, p % 2, s, :].bitcast(F32), op0=ALU.add, op1=ALU.subtract)
                last.then_inc(j_lo, 1)

            def k_lo(p, b):
                ps = pair_bank("k", p, b)
                dve.wait_ge(j_hi, j_index(("k", p), b) + 1)
                for s in range(2):
                    own = slice(0, HD) if s == 0 else slice(HD, P)
                    last = dve.scalar_tensor_tensor(
                        out=kst[own, p % 2, s, 1, :], in0=ps[own, :],
                        scalar=bqk_s[own, NPAIR + p:NPAIR + p + 1],
                        in1=kst[own, p % 2, s, 0, :].bitcast(F32), op0=ALU.add, op1=ALU.subtract)
                last.then_inc(j_lo, 1)

            def v_lo(t, b):
                bank = j_bank(("v", t))
                dve.wait_ge(j_hi, j_index(("v", t), b) + 1)
                dve.tensor_tensor(v[:, t, :, HD:2 * HD], ps_j[bank][:, :].rearrange("p (h c) -> p h c", h=NH),
                                  v[:, t, :, 0:HD].bitcast(F32), ALU.subtract).then_inc(j_lo, 1)

            def scores_max(h, b):
                H, q = 8 * b + h, h % 2
                dve.wait_ge(held, 1 + H)
                dve.wait_ge(s_done, H + 1)
                dve.memset(hold[:, 0:1], 0.0).then_inc(held, 1)
                m = maskf[:, :].bitcast(U32)
                diag = ps_s[:, 384:1536].rearrange("p (i c) -> p i c", c=384)[:, :, 0:P]
                dve.copy_predicated(diag, m.unsqueeze(1).to_broadcast([P, 3, P]),
                                    masked[:, :].unsqueeze(1).to_broadcast([P, 3, P])).then_inc(mask_done, 1)
                dve.copy_predicated(ps_s[:, 896:1024], m, masked[:, :].to_broadcast([P, P])).then_inc(mask_done, 1)
                dve.wait_ge(mask_done, 2 * H + 2)
                for i in range(NT):
                    last = dve.tensor_reduce(nm[:, q, i:i + 1], ps_s[:, S_OFF[i]:S_OFF[i] + (i + 1) * P],
                                             AX.X, ALU.max, negate=True)
                last.then_inc(max_done, 1)
                dve.wait_ge(max_done, H + 1)
                dve.tensor_scalar(nm[:, q, 0:3], nm[:, q, 0:3], -MASKED, None, ALU.min).then_inc(nm_ready, 1)

            def reciprocal(h, b):
                dve.wait_ge(den_ready, 8 * b + h + 1)
                dve.reciprocal(rden[:, h % 2, :], den[:, h % 2, :]).then_inc(rden_ready, 1)

            def vals_sum(h, b):
                H = 8 * b + h
                dve.wait_ge(vlo_done, H + 1)
                dve.wait_ge(vals_stored, 16 + 16 * H)
                dve.scalar_tensor_tensor(out=vt[0:HD, :], in0=ps_v[0:HD, :], scalar=bv_s[:, h:h + 1],
                                         in1=vt[HD:P, :], op0=ALU.add, op1=ALU.add).then_inc(vals_ready, 1)

            def next_low(n):
                _, _, raw_place, hi, lo = W.chunks[n]
                dve.wait_ge(next_hi, n + 1)
                dve.tensor_tensor(lo, raw_place, hi.bitcast(F32), ALU.subtract).then_inc(next_lo, 1)

            def first_vals_low():
                dve.wait_ge(v_first_hi, 1)
                dve.tensor_tensor(W.vl[:, :, :, :], W.vraw[:, :, :, :], W.vh[:, :, :, :].bitcast(F32), ALU.subtract)\
                    .then_inc(v_first_lo, 1)

            def lows(h, part, b, last):
                for kind, p, row, ks in between(h, part, b, last):
                    if ks is not FIRST:
                        {"q": q_lo, "k": k_lo, "v": v_lo, "x": x_lo}[kind](p, row)

            def body(b, last):
                for h in range(SLOTS):
                    if h < NH:
                        scores_max(h, b)
                    lows(h, 0, b, last)
                    if h == 5 and not last:
                        layernorm_stats(3, b + 1)
                    if h >= 2:
                        vals_sum(h - 2, b)
                    if 1 <= h <= NH:
                        for g in range(2):
                            p_lo(h - 1, g, b)
                    if h < NH:
                        reciprocal(h, b)
                    lows(h, 1, b, last)
                    if 1 <= h <= NH:
                        p_lo(h - 1, 2, b)
                    if last and h == 6:
                        first_vals_low()
                    if last:
                        for n in SPLITS.get(h, ()):
                            next_low(n)
                    if not last:
                        if h < 3:
                            layernorm_stats(h, b + 1)

            def split_w(n):
                dve.wait_ge(w_hi, n + 1)
                dve.tensor_tensor(w_chunk(n, wl), raw_chunk(n), w_chunk(n, wh).bitcast(F32), ALU.subtract)\
                    .then_inc(w_ready, 1)

            for t in range(3):
                layernorm_stats(t, 0)
            layernorm_stats(3, 0)
            x_lo(0, 0)
            x_lo(1, 0)
            x_lo(2, 0)
            split_w(0)
            x_lo(3, 0)
            for n in range(1, KD + 2):
                split_w(n)
            dve.wait_ge(bias_landed, 32)
            dve.wait_ge(consts, 14)
            k_lo(0, 0)
            q_lo(0, 0)
            for n in range(KD + 2, len(W_CHUNKS)):
                split_w(n)
            k_lo(1, 0)
            q_lo(1, 0)
            with dve.Fori(0, NB - 1) as b:
                body(b, False)
            body(NB - 1, True)

        @block.scalar
        def _(act):
            def x_hi(t, b):
                for g in range(2):
                    act.wait_ge(j_full[g], j_uses(("x", t, g), b))
                    act.activation(xTh[:, 4 * g:4 * g + 4, t * P:(t + 1) * P],
                                   x_bank(t, g, b)[:, :].rearrange("p (k t) -> p k t", k=4), ACT.Copy)\
                        .then_inc(j_hi, 1)

            def p_hi(h, g, b):
                o, n = PT_GROUP[g]
                act.wait_ge(t_full[g % 2], 2 * (8 * b + h) + g // 2 + 1)
                act.activation(PTh[:, o:o + n], ps_t[g % 2][:, 0:n], ACT.Copy).then_inc(t_hi, 1)

            def masked_spread(h, b):
                act.wait_ge(t_full[1], 2 * (8 * b + h) + 2)
                act.activation(WT[:, :], ps_t[1][:, 0:3 * P], ACT.Copy).then_inc(wt_ready, 1)

            def q_hi(p, b):
                bank, ps = j_bank(("q", p)), pair_bank("q", p, b)
                act.wait_ge(j_full[bank], j_uses(("q", p), b))
                for s in range(2):
                    own = slice(0, HD) if s == 0 else slice(HD, P)
                    last = act.activation(qst[own, p % 2, s, :], ps[own, :], ACT.Identity,
                                          bias=bqk_s[own, p:p + 1])
                last.then_inc(j_hi, 1)

            def k_hi(p, b):
                bank, ps = j_bank(("k", p)), pair_bank("k", p, b)
                act.wait_ge(j_full[bank], j_uses(("k", p), b))
                for s in range(2):
                    own = slice(0, HD) if s == 0 else slice(HD, P)
                    last = act.activation(kst[own, p % 2, s, 0, :], ps[own, :], ACT.Identity,
                                          bias=bqk_s[own, NPAIR + p:NPAIR + p + 1])
                last.then_inc(j_hi, 1)

            def v_hi(t, b):
                bank = j_bank(("v", t))
                act.wait_ge(j_full[bank], j_uses(("v", t), b))
                act.activation(v[:, t, :, 0:HD], ps_j[bank][:, :].rearrange("p (h c) -> p h c", h=NH), ACT.Copy)\
                    .then_inc(j_hi, 1)

            def exps(h, b):
                H, q = 8 * b + h, h % 2
                act.wait_ge(nm_ready, H + 1)
                act.activation(wm[:, q, 0:3], nm[:, q, 0:3], ACT.Exp, bias=masked[:, :])
                for i in range(NT):
                    n = (i + 1) * P
                    last = act.activation(pr[:, q, S_OFF[i]:S_OFF[i] + n], ps_s[:, S_OFF[i]:S_OFF[i] + n], ACT.Exp,
                                          bias=nm[:, q, i:i + 1], accum_out=acc[:, q, i:i + 1])
                last.then_inc(exp_done, 1)

            def vals_lo_part(h, b):
                H = 8 * b + h
                act.wait_ge(pv_done, H + 1)
                act.wait_ge(vals_ready, 1 + H)
                act.activation(vt[HD:P, :], ps_v[HD:P, :], ACT.Copy).then_inc(vlo_done, 1)

            def next_high(n):
                what, _, raw_place, hi, _ = W.chunks[n]
                act.wait_ge(next_landed[n], 32 if what == "B" else 16)
                act.activation(hi, raw_place, ACT.Copy).then_inc(next_hi, 1)

            def first_vals_high():
                act.wait_ge(v_first_landed, 32)
                act.activation(W.vh[:, :, :, :], W.vraw[:, :, :, :], ACT.Copy).then_inc(v_first_hi, 1)

            def highs(h, part, b, last, kinds="qkvx"):
                for kind, p, row, ks in between(h, part, b, last):
                    if ks is not FIRST and kind in kinds:
                        {"q": q_hi, "k": k_hi, "v": v_hi, "x": x_hi}[kind](p, row)

            def body(b, last):
                for h in range(SLOTS):
                    bare = last and h >= BARE
                    highs(h, 0, b, last, "x")
                    if h < NH and not bare:
                        exps(h, b)
                    highs(h, 0, b, last, "qkv")
                    if h >= 2:
                        vals_lo_part(h - 2, b)
                    if 1 <= h <= NH:
                        for g in range(2):
                            p_hi(h - 1, g, b)
                    if h < NH and bare:
                        exps(h, b)
                    highs(h, 1, b, last)
                    if 1 <= h <= NH:
                        p_hi(h - 1, 2, b)
                        masked_spread(h - 1, b)
                    if last and h == 6:
                        first_vals_high()
                    if last:
                        for n in SPLITS.get(h, ()):
                            next_high(n)

            def split_w(n):
                act.wait_ge(w_landed[n % RAW], 16 * (n // RAW + 1))
                act.activation(w_chunk(n, wh), raw_chunk(n), ACT.Copy).then_inc(w_hi, 1)

            for t in range(3):
                x_hi(t, 0)
            split_w(0)
            x_hi(3, 0)
            for n in range(1, KD + 2):
                split_w(n)
            act.wait_ge(bias_landed, 32)
            act.wait_ge(consts, 14)
            k_hi(0, 0)
            q_hi(0, 0)
            for n in range(KD + 2, len(W_CHUNKS)):
                split_w(n)
            k_hi(1, 0)
            q_hi(1, 0)
            with act.Fori(0, NB - 1) as b:
                body(b, False)
            body(NB - 1, True)

        @block.tensor
        def _(pe):
            def bank_free(entry, b):
                n = j_index(entry, b)
                if not (isinstance(n, int) and n < 2):
                    pe.wait_ge(j_lo, n - 1)

            def transpose_x(t, b):
                at = x_tile(t, b)
                pe.wait_ge(xn_ready, 4 * b + t + 1)
                for g in range(2):
                    if not (isinstance(b, int) and b == 0):
                        bank_free(("x", t, g), b)
                    elif t >= 2:
                        pe.wait_ge(j_lo, 2 * t + g - 3)
                    for k in range(4):
                        last = pe.transpose(x_bank(t, g, b)[:, k * P:(k + 1) * P],
                                            at[:, (4 * g + k) * P:(4 * g + k + 1) * P], ident[:, :])
                    last.then_inc(j_full[g], 1)

            def project(kind, p, b, ks):
                bank = j_bank((kind, p))
                ps = pair_bank(kind, p, b)
                if 0 in ks and ps is ps_j[bank]:
                    bank_free((kind, p), b)
                c = (kind == "k") * PART + p * P
                for k in ks:
                    if (kind, p) == ("k", 0) and k in (0, 4):
                        pe.wait_ge(j_lo, j_index(("x", 3, k // 4), b) + 1)
                    for w, xT in ((wh, xTh), (wh, xTl), (wl, xTh)):
                        last = pe.matmul(ps[:, :], w[:, k, c:c + P], xT[:, k, :],
                                         start=(k == 0 and w is wh and xT is xTh), stop=(k == KD - 1 and w is wl),
                                         skip_group_check=True)
                if KD - 1 in ks:
                    last.then_inc(j_full[bank], 1)

            def project_v(t, b):
                bank = j_bank(("v", t))
                bank_free(("v", t), b)
                for k in range(KD):
                    for xT, w in ((xTh, wh), (xTh, wl), (xTl, wh)):
                        last = pe.matmul(ps_j[bank][:, :], xT[:, k, t * P:(t + 1) * P], w[:, k, 2 * PART:3 * PART],
                                         start=(k == 0 and xT is xTh and w is wh), stop=(k == KD - 1 and xT is xTl))
                last.then_inc(j_full[bank], 1)

            def scores(h, b):
                H, p, s = 8 * b + h, h // 2, h % 2
                if h % 2 == 0:
                    pe.wait_ge(j_lo, j_index(("q", p), b) + 1)
                    pe.wait_ge(k_dup[p % 2], 32 * (2 * b + p // 2 + 1))
                if h > 0:
                    pe.wait_ge(exp_done, H)
                for i in range(NT):
                    for part in range(2):
                        last = pe.matmul(ps_s[:, S_OFF[i]:S_OFF[i] + (i + 1) * P],
                                         qst[:, p % 2, s, i * P:(i + 1) * P],
                                         kst[:, p % 2, s, part, 0:(i + 1) * P],
                                         start=(part == 0), stop=(part == 1), skip_group_check=True)
                last.then_inc(s_done, 1)

            def transpose_p(h, g, b):
                bank, H = g % 2, 8 * b + h
                if g >= 2:
                    pe.wait_ge(t_lo, 3 * H + g - 1)
                elif g == 0 and h > 0:
                    pe.wait_ge(t_lo, 3 * H)
                elif g == 1 and h > 0:
                    pe.wait_ge(wt_ready, H)
                if g == 0:
                    pe.wait_ge(p_ready, H + 1)
                if g == 3:
                    pe.wait_ge(d_ready, H + 1)
                    pe.matmul(ps_t[bank][:, 0:3 * P], ones[:, :], Dw[:, :], start=True, stop=True)\
                        .then_inc(t_full[bank], 1)
                    return
                o, n = PT_GROUP[g]
                for i, j, at in PT_BLOCKS:
                    if o <= at < o + n:
                        last = pe.transpose(ps_t[bank][:, at - o:at - o + P],
                                            pr[:, h % 2, S_OFF[i] + j * P:S_OFF[i] + (j + 1) * P], ident[:, :])
                last.then_inc(t_full[bank], 1)

            def values(h, b):
                H = 8 * b + h
                pe.wait_ge(t_lo, 3 * H + 3)
                if h == 0:
                    pe.wait_ge(j_lo, j_index(("v", 3), b) + 1)
                pe.wait_ge(wt_ready, H + 1)
                pe.wait_ge(vals_ready, 1 + H)
                for j in range(NT):
                    n = (NT - j) * P
                    for PT in (PTh, PTl):
                        pe.matmul(ps_v[:, j * P:], v[:, j, h, :], PT[:, PT_OFF[j]:PT_OFF[j] + n],
                                  start=(j == 0 and PT is PTh), stop=False, skip_group_check=True)
                    if j > 0:
                        last = pe.matmul(ps_v[:, 0:j * P], v[:, j, h, :], WT[:, 0:j * P],
                                         start=False, stop=(j == NT - 1), skip_group_check=True)
                last.then_inc(pv_done, 1)

            def first_output(half):
                pe.wait_ge(next_lo, W.KV)
                pe.wait_ge(v_first_lo, 1)
                for k in range(W.KV):
                    for a, w in ((W.vh, W.woh), (W.vh, W.wol), (W.vl, W.woh)):
                        pe.matmul(ps_j[half][:, :], a[:, 0, k, :], w[:, k, 512 * half:512 * half + 512],
                                  start=(k == 0 and a is W.vh and w is W.woh), stop=(k == W.KV - 1 and a is W.vl))

            def step(kind, p, b, ks):
                if kind == "x":
                    transpose_x(p, b)
                elif kind == "v":
                    project_v(p, b)
                else:
                    project(kind, p, b, ks)

            def body(b, last):
                ahead = () if last else AHEAD
                for h in range(SLOTS):
                    if h < NH and h not in ahead:
                        scores(h, b)
                    for args in between(h, 0, b, last):
                        step(*args)
                    if last and h == 9:
                        first_output(1)
                    if h >= 2:
                        values(h - 2, b)
                    if 1 <= h <= NH:
                        transpose_p(h - 1, 0, b)
                        transpose_p(h - 1, 1, b)
                    for args in between(h, 1, b, last):
                        step(*args)
                    if last and h == 8:
                        first_output(0)
                    if h + 1 in ahead:
                        scores(h + 1, b)
                    if 1 <= h <= NH:
                        transpose_p(h - 1, 2, b)
                        transpose_p(h - 1, 3, b)

            pe.wait_ge(consts, 14)
            for t in range(NT):
                transpose_x(t, 0)
            pe.wait_ge(j_lo, len(EARLY) - 4)
            for k in range(KD):
                pe.wait_ge(w_ready, k + 1)
                for kind in ("k", "q"):
                    project(kind, 0, 0, range(k, k + 1))
            project("k", 1, 0, WHOLE)
            project("q", 1, 0, WHOLE)
            pe.wait_ge(w_ready, len(W_CHUNKS))
            with pe.Fori(0, NB - 1) as b:
                body(b, False)
            body(NB - 1, True)


def output_phase(nc, x, valsT, vals_stored, ps_o, W, bf, gb, out):
    NB, S, D = x.shape
    PART = valsT.shape[1]
    R = W.R
    RANKS = (8, 16, 32, 64)
    NG = len(RANKS)
    NAG = W.wagh.shape[2]
    GW = NAG // 3
    assert 3 * GW == NAG and GW <= 512 and 2 * GW < D
    U0 = D - 2 * GW
    G0 = U0 + R
    BANK_COLS = [(0, GW), (GW, 2 * GW), (2 * GW, D)]
    BANK_ORDER = (2, 0, 1)
    KD = D // P
    KV = PART // P
    H = 512

    with ExitStack() as ctx:
        def sb(name, shape, dt, c=ctx):
            return c.enter_context(nc.sbuf_tensor(name, shape, dt))

        def sem(name):
            return ctx.enter_context(nc.semaphore(name))

        sb("weights_room", [P, W.floats], F32)
        wagh, wagl, woh, wol, Bh, Bl = W.wagh, W.wagl, W.woh, W.wol, W.Bh, W.Bl
        vraw, vh, vl, xs, bo_s = W.vraw, W.vh, W.vl, W.xs, W.bo_s
        y = sb("y", [P, D], F32)
        z = sb("z", [P, D], F32)
        x1 = sb("x1", [P, 2, D], F32)
        x2n = sb("x2n", [P, D], F32)
        x2Th = sb("x2Th", [P, KD, P], F32R)
        x2Tl = sb("x2Tl", [P, KD, P], F32R)
        bf_s = sb("bf_s", [P, D], F32)
        gb_s = sb("gb_s", [P, NG], F32)
        ident = sb("ident2", [P, P], F32)
        scores = sb("scores", [P, NG], F32)
        pmax = sb("pmax", [P, 2], F32)
        tmax = sb("tmax", [P, 2], F32)
        keep = sb("keep", [P, NG], F32)
        um = sb("um", [P, R], F32)
        us = sb("us", [P, 2 * R], F32)
        uT = sb("uT", [P, P], F32R)
        stats = sb("stats2", [P, 3, 12], F32)
        mv = sb("mv2", [P, 3, 2], F32)
        var_eps = sb("var_eps2", [P, 3], F32)
        rstd = sb("rstd2", [P, 3], F32)
        shift = sb("shift", [P, 3], F32)
        mhalf = sb("mhalf2", [P, 1], F32)
        eps = sb("eps2", [P, 1], F32)
        hold = sb("hold2", [1, 10], F32)
        f = sb("f", [P, D], F32)
        zf = sb("zf", [P, D], F32)
        outs = sb("outs", [P, 2, D], F32)

        ps_f = ctx.enter_context(nc.psum_tensor("ps_f", [P, 3, 512], F32))
        ps_x = ctx.enter_context(nc.psum_tensor("ps_x", [P, 2, 512], F32))
        ps_u = ctx.enter_context(nc.psum_tensor("ps_u", [P, 512], F32))

        bias_landed = sem("bias2_landed")
        w_hi = sem("w2_hi")
        w_ready = sem("w2_ready")
        v_landed = [sem(f"v_landed{i}") for i in range(2)]
        x_landed = [sem(f"xt_landed{i}") for i in range(2)]
        consts = sem("consts2")
        v_hi = sem("v_hi")
        v_ready = sem("v_ready")
        o_full = sem("o_full")
        y_done = sem("y_done")
        mv_ready = [sem(f"mv_ready{i}") for i in range(3)]
        ln_ready = [sem(f"ln_ready{i}") for i in range(3)]
        z_done = sem("z_done")
        x1_done = sem("x1_done")
        x2n_ready = sem("x2n_ready")
        x2_full = sem("x2_full")
        x2_hi = sem("x2_hi")
        x2_lo = sem("x2_lo")
        u_full = sem("u_full")
        us_ready = sem("us_ready")
        ut_full = sem("ut_full")
        ut_ready = sem("ut_ready")
        f_full = sem("f_full")
        f_done = sem("f_done")
        zf_done = sem("zf_done")
        out_done = sem("out_done")
        out_stored = [sem(f"out_stored{i}") for i in range(2)]

        xf = x.rearrange("b s d -> (b s) d")
        outf = out.rearrange("b s d -> (b s) d")
        late = range(W.SPLIT_EARLY, len(W.chunks))

        block = ctx.enter_context(nc.Block())

        @block.sync
        def _(sp):
            def load_v(b, i):
                sp.dma_start(vraw[:, i % 2, :, :], vals_tile(valsT, b, i)).then_inc(v_landed[i % 2], 16)

            def load_x(b, i):
                sp.dma_start(xs[:, i % 2, :], xf[bass.ds(b * S + i * P, P), :]).then_inc(x_landed[i % 2], 16)

            def body(b, last):
                for i in range(4):
                    if not (last and i + 2 > 3):
                        sp.wait_ge(x1_done, 2 * (4 * b + i) + 4)
                        load_x(b, i + 2)
                    if not (last and i + 3 > 3):
                        sp.wait_ge(v_ready, 4 * b + i + 2)
                        load_v(b, i + 3)
                    sp.wait_ge(out_done, 2 + 2 * (4 * b + i + 1))
                    sp.dma_start(outf[bass.ds(b * S + i * P, P), :], outs[:, i % 2, :]).then_inc(out_stored[i % 2], 16)

            load_x(0, 1)
            sp.dma_start(bf_s[:, :], bf.partition_broadcast(P)).then_inc(bias_landed, 16)
            sp.dma_start(gb_s[:, :], gb.partition_broadcast(P)).then_inc(bias_landed, 16)
            sp.wait_ge(vals_stored, 16 + 16 * NB * valsT.shape[1] // 64)
            load_v(0, 2)
            with sp.Fori(0, NB - 1) as b:
                body(b, False)
            body(NB - 1, True)
            for q in range(2):
                sp.wait_ge(out_stored[q], 16 + 16 * 2 * NB)

        @block.gpsimd
        def _(pool):
            def layernorm_scale(c, n):
                pool.wait_ge(mv_ready[c], n + 1)
                pool.tensor_tensor(var_eps[:, c:c + 1], mv[:, c, 1:2], eps[:, :], ALU.add)
                pool.drain()
                pool.tensor_tensor(rstd[:, c:c + 1], var_eps[:, c:c + 1], mhalf[:, :], ALU.pow)
                pool.drain()
                pool.tensor_scalar(shift[:, c:c + 1], mv[:, c, 0:1], rstd[:, c:c + 1], -1.0, ALU.mult, ALU.mult)\
                    .then_inc(ln_ready[c], 1)

            def first_residual(b, i):
                n = 4 * b + i
                if not (isinstance(n, int) and n == 0):
                    pool.wait_ge(x_landed[i % 2], 16 * (2 * b + i // 2 + i % 2))
                for half in range(2):
                    pool.wait_ge(z_done, 2 * n + half + 1)
                    cols = slice(H * half, H * half + H)
                    pool.tensor_tensor(x1[:, i % 2, cols], xs[:, i % 2, cols], z[:, cols], ALU.add).then_inc(x1_done, 1)

            def second_residual(b, i):
                n = 4 * b + i
                pool.wait_ge(out_stored[i % 2], 16 + 16 * (2 * b + i // 2))
                for half in range(2):
                    pool.wait_ge(zf_done, 2 + 2 * n + half + 1)
                    cols = slice(H * half, H * half + H)
                    pool.tensor_tensor(outs[:, i % 2, cols], x1[:, i % 2, cols], zf[:, cols], ALU.add)\
                        .then_inc(out_done, 1)

            def body(b, last):
                for i in range(4):
                    if not (last and i == 3):
                        layernorm_scale(0, 4 * b + i + 1)
                        first_residual(b, i + 1)
                        layernorm_scale(1, 4 * b + i + 1)
                    layernorm_scale(2, 4 * b + i)
                    second_residual(b, i)

            pool.memset(ident[:, :], 0.0).then_inc(consts, 1)
            pool.memset(mhalf[:, :], -0.5).then_inc(consts, 1)
            pool.memset(eps[:, :], EPS).then_inc(consts, 1)
            pool.memset(keep[:, :], 1.0).then_inc(consts, 1)
            starts = ((o_full, 2), (v_hi, 2), (v_ready, 2), (zf_done, 2), (out_done, 2), (x2_full, 2), (x1_done, 2), (out_stored[0], 16),
                      (out_stored[1], 16), (f_done, 3))
            for at, (done, turn) in enumerate(starts):
                pool.memset(hold[:, at:at + 1], 0.0).then_inc(done, turn)
            pool.wait_ge(consts, 4)
            pool.affine_select(out=ident[:, :], in_=ident[:, :], compare_op=ALU.not_equal, fill=1.0, base=0,
                               pattern=[[-1, P]], channel_multiplier=1).then_inc(consts, 1)
            layernorm_scale(0, 0)
            first_residual(0, 0)
            layernorm_scale(1, 0)
            with pool.Fori(0, NB - 1) as b:
                body(b, False)
            body(NB - 1, True)

        @block.vector
        def _(dve):
            def half_statistics(c, t, i):
                dve.bn_stats(stats[:, c, 6 * i:6 * i + 6], t[:, H * i:H * i + H])

            def mean_and_variance(c):
                dve.drain()
                dve.bn_aggr(mv[:, c, :], stats[:, c, :]).then_inc(mv_ready[c], 1)

            def attention_out(n):
                if not (isinstance(n, int) and n == 0):
                    dve.wait_ge(z_done, 2 * n)
                for half in range(2):
                    dve.wait_ge(o_full, 2 * n + half + 1)
                    dve.tensor_tensor(y[:, H * half:H * half + H], ps_o[:, half, :], bo_s[:, H * half:H * half + H],
                                      ALU.add).then_inc(y_done, 1)
                    dve.drain()
                    half_statistics(0, y, half)
                mean_and_variance(0)

            def route(n):
                dve.wait_ge(u_full, n + 1)
                dve.tensor_tensor(scores[:, :], ps_f[:, 2, G0:G0 + NG], gb_s[:, :], ALU.add)
                dve.drain()
                pairs = scores[:, :].rearrange("p (a c) -> p c a", c=2)
                dve.tensor_tensor(pmax[:, :], pairs[:, 0, :], pairs[:, 1, :], ALU.max)
                dve.drain()
                dve.tensor_tensor(tmax[:, 0:1], pmax[:, 1:2], scores[:, 1:2], ALU.max)
                dve.tensor_tensor(tmax[:, 1:2], pmax[:, 0:1], scores[:, 2:3], ALU.max)
                dve.drain()
                dve.tensor_tensor(keep[:, 1:2], tmax[:, 0:1], scores[:, 0:1], ALU.is_gt)
                dve.tensor_tensor(keep[:, 2:3], pmax[:, 1:2], pmax[:, 0:1], ALU.is_gt)
                dve.tensor_tensor(keep[:, 3:4], scores[:, 3:4], tmax[:, 1:2], ALU.is_gt)
                dve.drain()
                for r, (lo, hi) in enumerate(zip((0,) + RANKS, RANKS)):
                    dve.tensor_scalar(um[:, lo:hi], ps_f[:, 2, U0 + lo:U0 + hi], keep[:, r:r + 1], None, ALU.mult)
                dve.drain()
                dve.tensor_copy(us[:, 0:R].bitcast(F32R), um[:, :])
                dve.drain()
                dve.tensor_tensor(us[:, R:2 * R].bitcast(F32R), um[:, :], us[:, 0:R], ALU.subtract)\
                    .then_inc(us_ready, 1)

            def second_layernorm(b, i):
                for half in range(2):
                    dve.wait_ge(x1_done, 2 * (4 * b + i) + 2 + half + 1)
                    half_statistics(1, x1[:, i % 2, :], half)
                mean_and_variance(1)

            def x2_low(n):
                for g in range(2):
                    dve.wait_ge(x2_hi, 2 * n + g + 1)
                    dve.tensor_tensor(x2Tl[:, 4 * g:4 * g + 4, :],
                                      ps_x[:, g, :].rearrange("p (k t) -> p k t", k=4),
                                      x2Th[:, 4 * g:4 * g + 4, :].bitcast(F32), ALU.subtract).then_inc(x2_lo, 1)

            def v_low(b, i):
                dve.wait_ge(v_hi, 4 * b + i + 1)
                dve.tensor_tensor(vl[:, i % 2, :, :], vraw[:, i % 2, :, :], vh[:, i % 2, :, :].bitcast(F32),
                                  ALU.subtract).then_inc(v_ready, 1)

            def ffn_out(n):
                dve.wait_ge(zf_done, 2 + 2 * n)
                for m, g in enumerate(BANK_ORDER):
                    lo, hi = BANK_COLS[g]
                    dve.wait_ge(f_full, 3 * n + m + 1)
                    dve.tensor_tensor(f[:, lo:hi], ps_f[:, g, 0:hi - lo], bf_s[:, lo:hi], ALU.add).then_inc(f_done, 1)
                dve.drain()
                for half in range(2):
                    half_statistics(2, f, half)
                mean_and_variance(2)

            def body(b, last):
                for i in range(4):
                    n, more = 4 * b + i, not (last and i == 3)
                    if more:
                        attention_out(n + 1)
                    route(n)
                    if not (last and i + 2 > 3):
                        v_low(b, i + 2)
                    if more:
                        second_layernorm(b, i + 1)
                        x2_low(n + 1)
                    ffn_out(n)

            def split_w(n):
                _, _, raw_place, hi, lo = W.chunks[n]
                dve.wait_ge(w_hi, n - W.SPLIT_EARLY + 1)
                dve.tensor_tensor(lo, raw_place, hi.bitcast(F32), ALU.subtract).then_inc(w_ready, 1)

            attention_out(0)
            for n in late[:3]:
                split_w(n)
            second_layernorm(0, 0)
            for n in late[3:]:
                split_w(n)
            x2_low(0)
            dve.wait_ge(bias_landed, 32)
            dve.wait_ge(consts, 5)
            with dve.Fori(0, NB - 1) as b:
                body(b, False)
            body(NB - 1, True)

        @block.scalar
        def _(act):
            def scaled(out_, in_, c):
                return act.activation(out_, in_, ACT.Identity, scale=rstd[:, c:c + 1], bias=shift[:, c:c + 1])

            def first_norm(n):
                act.wait_ge(ln_ready[0], n + 1)
                for half in range(2):
                    act.wait_ge(x1_done, 2 * n + half + 1)
                    cols = slice(H * half, H * half + H)
                    scaled(z[:, cols], y[:, cols], 0).then_inc(z_done, 1)

            def second_norm(b, i):
                n = 4 * b + i
                act.wait_ge(x2_full, 2 + 2 * n)
                act.wait_ge(ln_ready[1], n + 1)
                for half in range(2):
                    cols = slice(H * half, H * half + H)
                    scaled(x2n[:, cols], x1[:, i % 2, cols], 1).then_inc(x2n_ready, 1)

            def x2_high(n):
                for g in range(2):
                    act.wait_ge(x2_full, 2 + 2 * n + g + 1)
                    act.activation(x2Th[:, 4 * g:4 * g + 4, :], ps_x[:, g, :].rearrange("p (k t) -> p k t", k=4),
                                   ACT.Copy).then_inc(x2_hi, 1)

            def v_high(b, i):
                if not (isinstance(b, int) and 4 * b + i < 2):
                    act.wait_ge(v_landed[i % 2], 16 * (2 * b + i // 2))
                    act.wait_ge(o_full, 2 * (4 * b + i) - 2)
                act.activation(vh[:, i % 2, :, :], vraw[:, i % 2, :, :], ACT.Copy).then_inc(v_hi, 1)

            def u_transposed(n):
                act.wait_ge(ut_full, n + 1)
                act.activation(uT[:, :], ps_u[:, 0:P], ACT.Copy).then_inc(ut_ready, 1)

            def last_norm(n):
                act.wait_ge(ln_ready[2], n + 1)
                act.wait_ge(out_done, 2 + 2 * n)
                for half in range(2):
                    cols = slice(H * half, H * half + H)
                    scaled(zf[:, cols], f[:, cols], 2).then_inc(zf_done, 1)

            def body(b, last):
                for i in range(4):
                    n, more = 4 * b + i, not (last and i == 3)
                    if not (last and i + 2 > 3):
                        v_high(b, i + 2)
                    if more:
                        first_norm(n + 1)
                    u_transposed(n)
                    if more:
                        second_norm(b, i + 1)
                        x2_high(n + 1)
                    last_norm(n)

            def split_w(n):
                _, _, raw_place, hi, lo = W.chunks[n]
                act.activation(hi, raw_place, ACT.Copy).then_inc(w_hi, 1)

            for n in late[:4]:
                split_w(n)
            first_norm(0)
            for n in late[4:]:
                split_w(n)
            second_norm(0, 0)
            x2_high(0)
            with act.Fori(0, NB - 1) as b:
                body(b, False)
            body(NB - 1, True)

        @block.tensor
        def _(pe):
            def attention_product(b, i):
                n = 4 * b + i
                pe.wait_ge(v_ready, n + 1)
                for half in range(2):
                    if not (isinstance(n, int) and n == 0):
                        pe.wait_ge(y_done, 2 * n - 1 + half)
                    cols = slice(H * half, H * half + H)
                    for k in range(KV):
                        for a, w in ((vh, woh), (vh, wol), (vl, woh)):
                            last = pe.matmul(ps_o[:, half, :], a[:, i % 2, k, :], w[:, k, cols],
                                             start=(k == 0 and a is vh and w is woh), stop=(k == KV - 1 and a is vl))
                    last.then_inc(o_full, 1)

            def transpose_x2(n):
                for g in range(2):
                    pe.wait_ge(x2n_ready, 2 * n + g + 1)
                    if not (isinstance(n, int) and n == 0):
                        pe.wait_ge(x2_lo, 2 * n - 1 + g)
                    for k in range(4):
                        last = pe.transpose(ps_x[:, g, k * P:(k + 1) * P], x2n[:, (4 * g + k) * P:(4 * g + k + 1) * P],
                                            ident[:, :])
                    last.then_inc(x2_full, 1)

            def ffn(n):
                pe.wait_ge(x2_lo, 2 * n + 2)
                pe.wait_ge(f_done, 3 + 3 * n)
                for g in BANK_ORDER:
                    cols = slice(GW * g, GW * g + GW)
                    for k in range(KD):
                        for a, w in ((x2Th, wagh), (x2Th, wagl), (x2Tl, wagh)):
                            last = pe.matmul(ps_f[:, g, 0:GW], a[:, k, :], w[:, k, cols],
                                             start=(k == 0 and a is x2Th and w is wagh), stop=False,
                                             skip_group_check=True)
                    if g == 2:
                        last.then_inc(u_full, 1)
                    if g == 0:
                        pe.wait_ge(us_ready, n + 1)
                        pe.transpose(ps_u[:, 0:P], us[:, :], ident[:, :]).then_inc(ut_full, 1)
                pe.wait_ge(ut_ready, n + 1)
                for g in BANK_ORDER:
                    lo, hi = BANK_COLS[g]
                    for Bp in (Bh, Bl):
                        last = pe.matmul(ps_f[:, g, 0:hi - lo], uT[:, :], Bp[:, lo:hi], start=False,
                                         stop=(Bp is Bl), skip_group_check=True)
                    last.then_inc(f_full, 1)

            def body(b, last):
                for i in range(4):
                    n, more = 4 * b + i, not (last and i == 3)
                    ffn(n)
                    if more:
                        transpose_x2(n + 1)
                    if not (last and i + 2 > 3):
                        attention_product(b, i + 2)

            attention_product(0, 1)
            pe.wait_ge(consts, 5)
            transpose_x2(0)
            pe.wait_ge(w_ready, len(late))
            with pe.Fori(0, NB - 1) as b:
                body(b, False)
            body(NB - 1, True)


def build(nc, valsT, out, x, wqkvT, bqk, bv, woT, bo, wagT, bf, gb, BT):
    with ExitStack() as room:
        W = OutputWeights(nc, room, *x.shape, woT.shape[0], BT.shape[0], wagT.shape[1])
    with nc.semaphore("vals_stored") as vals_stored, nc.psum_tensor("ps_o", [P, 2, 512], F32) as ps_o:
        attention_phase(nc, x, wqkvT, bqk, bv, valsT, vals_stored, ps_o, W, woT, bo, wagT, BT)
        output_phase(nc, x, valsT, vals_stored, ps_o, W, bf, gb, out)


def kernel(L0_attn_x, L0_attn_w_qkv, L0_attn_b_qkv, L0_attn_w_o, L0_attn_b_o, L0_ffn_W, L0_ffn_b, L0_ffn_A,
           L0_ffn_B, L0_ffn_gate_w, L0_ffn_gate_b):
    import numpy as np
    import concourse.bacc as bacc
    from concourse.bass_utils import run_bass_kernel_spmd

    c = np.ascontiguousarray
    x = np.asarray(L0_attn_x)
    b_qkv = np.asarray(L0_attn_b_qkv)
    part = b_qkv.shape[0] // 3
    arrays = {
        "x": c(x),
        "wqkvT": c(np.asarray(L0_attn_w_qkv).T),
        "bqk": c(b_qkv[:2 * part].reshape(-1, P).T),
        "bv": c(b_qkv[2 * part:].reshape(-1, 64).T),
        "woT": c(np.asarray(L0_attn_w_o).T),
        "bo": c(L0_attn_b_o),
        "wagT": c(np.concatenate([np.asarray(L0_ffn_W).T, np.asarray(L0_ffn_A).T, np.asarray(L0_ffn_gate_w).T], axis=1)),
        "bf": c(L0_ffn_b),
        "gb": c(L0_ffn_gate_b),
        "BT": c(np.asarray(L0_ffn_B).T),
    }
    nc = bacc.Bacc("TRN2", target_bir_lowering=False, num_devices=1)
    aps = {k: nc.dram_tensor(f"in_{k}", a.shape, mybir.dt.from_np(a.dtype), kind="ExternalInput").ap()
           for k, a in arrays.items()}
    valsT = nc.dram_tensor("valsT", (x.shape[0], part, x.shape[1]), F32, kind="Internal").ap()
    out = nc.dram_tensor("out", x.shape, F32, kind="ExternalOutput").ap()
    build(nc, valsT, out, **aps)
    r = run_bass_kernel_spmd(nc, [{f"in_{k}": a for k, a in arrays.items()}], core_ids=[0])
    return r.results[0]["out"]
```
